# Optimizing a Trainium2 kernel written in Bass

```python
import numpy as np
import jax
import jax.numpy as jnp

def _softmax(x, axis=-1):
    return jax.nn.softmax(x, axis=axis)

def _gelu(x):
    return jax.nn.gelu(x, approximate=True)

def _silu(x):
    return jax.nn.silu(x)

def _sigmoid(x):
    return jax.nn.sigmoid(x)

def _layernorm(x, axis=-1, eps=1e-05):
    m = jnp.mean(x, axis=axis, keepdims=True)
    v = jnp.var(x, axis=axis, keepdims=True)
    return (x - m) / jnp.sqrt(v + eps)

def _scatter_add(tgt, idx, src, axis=0):
    return tgt.at[idx].add(src)

def _segment_sum(src, seg, n):
    return jax.ops.segment_sum(src, seg, n)
kernel_name = 'mk_adj_preln_d2_adj_r2_bf4812'

def setup_inputs(seed: int=0):
    np.random.seed(seed)
    _w = jnp.asarray

    def _rec_inputs():
        import jax
        import jax.numpy as jnp
        _gk = jax.random.key(seed)
        x = -0.0005207 + 1.001 * jax.random.normal(jax.random.fold_in(_gk, 1), (8192, 128), jnp.float32)
        _a = jax.random.bernoulli(jax.random.fold_in(_gk, 2), 0.00195312, (8192, 8192))
        _a = jnp.logical_or(_a, jnp.swapaxes(_a, -1, -2))
        _a = jnp.logical_or(_a, jnp.eye(8192, dtype=bool))
        _af = _a.astype(jnp.float32)
        _af = _af * jax.random.uniform(jax.random.fold_in(_gk, 3), (8192, 8192), jnp.float32, 0.05, 1)
        adj = _af
        return (x, adj)
    x, adj = _rec_inputs()

    def _L0_gnn_setup():
        import jax, jax.numpy as jnp
        import numpy as np
        ALPHA = 0.1
        N, F = (8192, 128)
        key = jax.random.key(seed)
        k1, k2, k3 = jax.random.split(key, 3)
        x = jax.random.normal(k1, (N, F), dtype=jnp.float32)
        adj = jax.random.uniform(k2, (N, N), dtype=jnp.float32)
        h = jax.random.normal(k3, (N, F), dtype=jnp.float32)
        return {'x': x, 'adj': adj, 'h': h}
    _L0_gnn_all = _L0_gnn_setup()
    _L0_gnn_in = {k: v for k, v in _L0_gnn_all.items() if k in ('h',)}
    del _L0_gnn_all

    def _L1_gnn_setup():
        import jax, jax.numpy as jnp
        import numpy as np
        N, DIM = (8192, 128)

        def _gru_cell(x, h, W_ih, W_hh, b_ih, b_hh):
            gi = x @ W_ih.T + b_ih
            gh = h @ W_hh.T + b_hh
            i_r, i_z, i_n = jnp.split(gi, 3, axis=-1)
            h_r, h_z, h_n = jnp.split(gh, 3, axis=-1)
            r = jax.nn.sigmoid(i_r + h_r)
            z = jax.nn.sigmoid(i_z + h_z)
            n = jnp.tanh(i_n + r * h_n)
            return (1.0 - z) * n + z * h
        key = jax.random.key(seed)
        ks = jax.random.split(key, 8)
        states = jax.random.normal(ks[0], (N, DIM), dtype=jnp.float32)
        adj = jax.random.uniform(ks[1], (N, N), dtype=jnp.float32)
        s = 1.0 / np.sqrt(DIM)
        W_msg = jax.random.uniform(ks[2], (DIM, DIM), minval=-s, maxval=s, dtype=jnp.float32)
        b_msg = jax.random.uniform(ks[3], (DIM,), minval=-s, maxval=s, dtype=jnp.float32)
        W_ih = jax.random.uniform(ks[4], (3 * DIM, DIM), minval=-s, maxval=s, dtype=jnp.float32)
        W_hh = jax.random.uniform(ks[5], (3 * DIM, DIM), minval=-s, maxval=s, dtype=jnp.float32)
        b_ih = jax.random.uniform(ks[6], (3 * DIM,), minval=-s, maxval=s, dtype=jnp.float32)
        b_hh = jax.random.uniform(ks[7], (3 * DIM,), minval=-s, maxval=s, dtype=jnp.float32)
        return {'states': states, 'adj': adj, 'W_msg': W_msg, 'b_msg': b_msg, 'W_ih': W_ih, 'W_hh': W_hh, 'b_ih': b_ih, 'b_hh': b_hh}
    _L1_gnn_all = _L1_gnn_setup()
    _L1_gnn_in = {k: v for k, v in _L1_gnn_all.items() if k in ('W_msg', 'b_msg', 'W_ih', 'W_hh', 'b_ih', 'b_hh')}
    del _L1_gnn_all
    return {'x': x, 'adj': adj, 'L0_gnn_h': _L0_gnn_in['h'], 'L1_gnn_W_msg': _L1_gnn_in['W_msg'], 'L1_gnn_b_msg': _L1_gnn_in['b_msg'], 'L1_gnn_W_ih': _L1_gnn_in['W_ih'], 'L1_gnn_W_hh': _L1_gnn_in['W_hh'], 'L1_gnn_b_ih': _L1_gnn_in['b_ih'], 'L1_gnn_b_hh': _L1_gnn_in['b_hh']}

def reference(x, adj, L0_gnn_h, L1_gnn_W_msg, L1_gnn_b_msg, L1_gnn_W_ih, L1_gnn_W_hh, L1_gnn_b_ih, L1_gnn_b_hh):
    import jax
    import jax.numpy as jnp

    def _L0_gnn_ref(x, adj, h):
        import jax, jax.numpy as jnp
        import numpy as np
        ALPHA = 0.1
        N, F = (8192, 128)
        return (1.0 - ALPHA) * (adj @ x) + ALPHA * h

    def _L1_gnn_ref(states, adj, W_msg, b_msg, W_ih, W_hh, b_ih, b_hh):
        import jax, jax.numpy as jnp
        import numpy as np
        N, DIM = (8192, 128)

        def _gru_cell(x, h, W_ih, W_hh, b_ih, b_hh):
            gi = x @ W_ih.T + b_ih
            gh = h @ W_hh.T + b_hh
            i_r, i_z, i_n = jnp.split(gi, 3, axis=-1)
            h_r, h_z, h_n = jnp.split(gh, 3, axis=-1)
            r = jax.nn.sigmoid(i_r + h_r)
            z = jax.nn.sigmoid(i_z + h_z)
            n = jnp.tanh(i_n + r * h_n)
            return (1.0 - z) * n + z * h
        agg = adj @ states
        msg = jax.nn.relu(agg @ W_msg.T + b_msg)
        return _gru_cell(msg, states, W_ih, W_hh, b_ih, b_hh)
    h = jnp.maximum(_layernorm(x, axis=-1), 0.0)
    x = x + _L0_gnn_ref(h, adj, L0_gnn_h)
    h = jnp.maximum(_layernorm(x, axis=-1), 0.0)
    x = x + _L1_gnn_ref(h, adj, L1_gnn_W_msg, L1_gnn_b_msg, L1_gnn_W_ih, L1_gnn_W_hh, L1_gnn_b_ih, L1_gnn_b_hh)
    return x

_drawn_inputs = setup_inputs


def setup_inputs(seed=0):
    import zlib

    import numpy as np

    out = dict(_drawn_inputs(seed))
    spreads = {}
    factors = {'L0_gnn_h': 3.516,
     'L1_gnn_b_msg': 55.502,
     'L1_gnn_W_hh': 3.674,
     'L1_gnn_b_ih': 22.98,
     'L1_gnn_b_hh': 30.311}
    for name, (base, spread) in spreads.items():
        noise = np.random.default_rng([zlib.crc32(name.encode()), seed]).standard_normal(out[name].shape)
        drawn = base * np.exp(spread * noise) if base else spread * noise
        out[name] = jnp.asarray(drawn.astype(out[name].dtype))
    for name, factor in factors.items():
        out[name] = (out[name] * factor).astype(out[name].dtype)
    return out
```

```python
from contextlib import ExitStack

import concourse.bass as bass
from concourse import mybir

FP32 = mybir.dt.float32
FP32R = mybir.dt.float32r
ALU = mybir.AluOpType
ACT = mybir.ActivationFunctionType

P = 128
N = 8192
CH = 512
JT = 4
NC = N // CH
GW = JT * CH
RAW = 4
SPL = 2
XS = 8
HT = JT // 2
HALF = HT * CH
NH = 2 * SPL
HW = JT * P
NA = NC * NC
NB = NC * (NC + 1) // 2
ALPHA = 0.1
EPS = 1e-5
MSG, I_R, I_Z, I_N, H_R, H_Z, H_N = range(7)


def gnn_program(nc, adj, x_rows, x_cols, h_cols, weights, biases, identity, out):
    x2_spill = nc.dram_tensor("x2_spill", (NC, P, CH), FP32).ap()
    part_spill = nc.dram_tensor("part_spill", (NC, P, CH), FP32).ap()
    ctx = ExitStack()
    with ctx:
        at = [-(-nc.sbuf_base // 64) * 64]

        def place(name, shape, dtype=FP32, offset=None):
            size = 4
            for n in shape[1:]:
                size *= n
            if offset is None:
                offset, at[0] = at[0], at[0] + -(-size // 64) * 64
            return nc.alloc_sbuf_tensor_at(name, shape, dtype, offset=offset)

        h1_at = at[0]
        h1_hi = place("h1_hi", [P, NC, HW], FP32R)
        h1_lo = place("h1_lo", [P, NC, HW], FP32R)
        h2_hi = place("h2_hi", [P, NC, HW], FP32R)
        h2_lo_at = at[0]
        h2_lo = place("h2_lo", [P, NC, HW], FP32R)
        x_in = place("x_in", [P, NC, HW], offset=h2_lo_at)
        raw = place("raw", [P, RAW, GW])
        adj_hi = place("adj_hi", [P, SPL, GW], FP32R)
        adj_lo_at = at[0]
        adj_lo = place("adj_lo", [P, SPL, GW], FP32R)
        h1_now = place("h1_now", [P, 2, HW], offset=adj_lo_at + 4 * (SPL * GW - 2 * HW))
        ident = place("ident", [P, P])
        bias = place("bias", [P, 7])
        gate_bias = place("gate_bias", [P, 2])
        parts = place("parts", [P, 2, JT, 6])
        moments = place("moments", [P, 2, JT, 2])
        var_eps = place("var_eps", [P, 2, JT])
        rstd = place("rstd", [P, 2, JT])
        power = place("power", [P, JT])
        epsilon = place("epsilon", [P, JT])
        tenth = place("tenth", [P, 1])
        carrier = place("carrier", [P, 1])
        act_carrier = place("act_carrier", [P, 1])
        xc_in = place("xc_in", [P, CH])
        hc_in = place("hc_in", [P, CH])
        x_mix = place("x_mix", [P, CH])
        x2 = place("x2", [P, CH])
        normed = place("normed", [P, HW])
        part_out = place("part_out", [P, CH])
        assert at[0] <= nc.sbuf_usable_end
        at[0] = h1_at
        w_raw = place("w_raw", [P, 7, P])
        w_hi = place("w_hi", [P, 7, P], FP32R)
        w_lo = place("w_lo", [P, 7, P], FP32R)
        part_in = place("part_in", [P, CH])
        agg = place("agg", [P, CH])
        agg_hi = place("agg_hi", [P, CH], FP32R)
        agg_lo = place("agg_lo", [P, CH], FP32R)
        msg = place("msg", [P, CH])
        msg_hi = place("msg_hi", [P, CH], FP32R)
        msg_lo = place("msg_lo", [P, CH], FP32R)
        h2_sum = place("h2_sum", [P, HW])
        state = place("state", [P, CH])
        state_hi = place("state_hi", [P, CH], FP32R)
        state_lo = place("state_lo", [P, CH], FP32R)
        reset = place("reset", [P, CH])
        update = place("update", [P, CH])
        new = place("new", [P, CH])
        pre_a = place("pre_a", [P, CH])
        pre_b = place("pre_b", [P, CH])
        diff = place("diff", [P, CH])
        mixed = place("mixed", [P, CH])
        gru = place("gru", [P, CH])
        x2_in = place("x2_in", [P, CH])
        result = place("result", [P, CH])
        assert at[0] <= h1_at + 2 * 4 * NC * HW

        def bank(name, shape):
            return ctx.enter_context(nc.psum_tensor(name, shape, FP32))

        acc = bank("acc", [P, 2 * CH])
        acc2 = bank("acc2", [P, CH])
        turned = bank("turned", [P, CH])
        g_r = bank("g_r", [P, CH])
        g_z = bank("g_z", [P, CH])
        g_in = bank("g_in", [P, CH])
        g_hn = bank("g_hn", [P, CH])

        def sem(name):
            return ctx.enter_context(nc.semaphore(name))

        x_landed = [sem(f"x_landed{i}") for i in range(XS)]
        raw_landed = [sem(f"raw_landed{i}") for i in range(RAW)]
        const_landed = sem("const_landed")
        cols_landed = sem("cols_landed")
        cols_used = sem("cols_used")
        power_set = sem("power_set")
        hi_ready = sem("hi_ready")
        lo_ready = sem("lo_ready")
        adj_used = sem("adj_used")
        parts_ready = sem("parts_ready")
        moments_ready = sem("moments_ready")
        eps_added = sem("eps_added")
        rstd_ready = sem("rstd_ready")
        h1_now_ready = sem("h1_now_ready")
        normed_ready = sem("normed_ready")
        h_hi_ready = sem("h_hi_ready")
        h_ready = sem("h_ready")
        mix_half = sem("mix_half")
        mix_ready = sem("mix_ready")
        x2_ready = sem("x2_ready")
        x2_stored = sem("x2_stored")
        x2_turned = sem("x2_turned")
        part_ready = sem("part_ready")
        part_stored = sem("part_stored")
        w_landed = sem("w_landed")
        w_hi_ready = sem("w_hi_ready")
        w_ready = sem("w_ready")
        bias_ready = sem("bias_ready")
        part_landed = sem("part_landed")
        sum_ready = sem("sum_ready")
        state_turned = sem("state_turned")
        state_out = sem("state_out")
        state_hi_ready = sem("state_hi_ready")
        state_ready = sem("state_ready")
        agg_out = sem("agg_out")
        agg_hi_ready = sem("agg_hi_ready")
        agg_ready = sem("agg_ready")
        msg_done = sem("msg_done")
        msg_out = sem("msg_out")
        msg_hi_ready = sem("msg_hi_ready")
        msg_ready = sem("msg_ready")
        gates_done = sem("gates_done")
        reset_ready = sem("reset_ready")
        update_ready = sem("update_ready")
        pre_a_ready = sem("pre_a_ready")
        pre_ready = sem("pre_ready")
        new_ready = sem("new_ready")
        diff_ready = sem("diff_ready")
        mixed_ready = sem("mixed_ready")
        gru_ready = sem("gru_ready")
        x2_landed = sem("x2_landed")
        result_ready = sem("result_ready")
        out_stored = sem("out_stored")

        def row(t, k):
            return t[k] if isinstance(k, int) else t[bass.ds(k, 1)].rearrange("o p n -> (o p) n")

        def group(table, k):
            return table[:, k, :] if isinstance(k, int) else table[:, bass.ds(k, 1), :].rearrange("p o n -> p (o n)")

        def row_of(eng, turn):
            r = (turn // 2 + (turn % 2) * (NC - 1 - 2 * (turn // 2))) % NC
            return r if isinstance(turn, int) else eng.snap(r)

        def rows_of_pass_b(eng, name, split, first, second, third):
            last = eng.alloc_register(name + "_last")
            before = eng.alloc_register(name + "_before")
            first_at = eng.alloc_register(name + "_first_at")
            second_at = eng.alloc_register(name + "_second_at")
            third_at = eng.alloc_register(name + "_third_at")
            for register, value in ((last, 0), (before, 0), (first_at, NC), (second_at, NB), (third_at, NB)):
                eng.reg_mov(register, value)
            with eng.Fori(0, NB // RAW) as m4:
                for u in range(RAW):
                    m = RAW * m4 + u
                    split(m, u)
                    with eng.If(m == eng.snap(second_at)):
                        second(last, before)
                    with eng.If(m == eng.snap(third_at)):
                        third(last, before)
                        eng.reg_mov(before, eng.snap(last))
                        eng.reg_mov(last, eng.snap(last) + 1)
                    with eng.If(m == eng.snap(first_at)):
                        first(last, before, m)
                        blocks = eng.snap(NC - row_of(eng, eng.snap(last) + 1))
                        eng.reg_mov(second_at, m + 2 - (blocks < 2))
                        eng.reg_mov(third_at, m + 3 - (blocks < 2) - (blocks < 3))
                        eng.reg_mov(first_at, m + blocks)

        block = ctx.enter_context(nc.Block())

        @block.sync
        def _(sp):
            def load_x(q):
                sp.dma_start(x_in[:, q, :], x_rows[q]).then_inc(x_landed[q % XS], 16)

            def load_block(c, q):
                before = NC * c + q - RAW
                if isinstance(c, int):
                    if 0 <= before < NC:
                        sp.wait_ge(adj_used, 2 * (before + 1))
                    if before >= NC:
                        sp.wait_ge(lo_ready, 2 * (before - NC + 1))
                else:
                    sp.wait_ge(lo_ready, 2 * (before - NC + 1))
                sp.dma_start(raw[:, q % RAW, :], adj[NC * c + NC - 1 - q]).then_inc(raw_landed[q % RAW], 16)

            def load_cols(c):
                if not isinstance(c, int):
                    sp.wait_ge(mix_ready, c)
                sp.dma_start(xc_in[:, :], row(x_cols, c)).then_inc(cols_landed, 16)
                sp.dma_start(hc_in[:, :], row(h_cols, c)).then_inc(cols_landed, 16)

            def store_x2(k):
                sp.wait_ge(x2_ready, k + 1)
                sp.dma_start(row(x2_spill, k), x2[:, :]).then_inc(x2_stored, 16)

            def store_part(k):
                sp.wait_ge(part_ready, k)
                sp.dma_start(row(part_spill, k), part_out[:, :]).then_inc(part_stored, 16)

            for q in range(4):
                load_x(q)
            for q in range(NC):
                load_block(0, q)
                if q + 4 < NC:
                    load_x(q + 4)
            load_cols(0)
            sp.dma_start(ident[:, :], identity).then_inc(const_landed, 16)
            sp.dma_start(bias[:, :], biases).then_inc(const_landed, 16)

            def chunk(c):
                for q in range(NC):
                    load_block(c, q)
                    if q == 6:
                        store_x2(c - 1)
                        if not isinstance(c, int):
                            store_part(c - 1)
                    if q == 8:
                        load_cols(c)

            chunk(1)
            with sp.Fori(2, NC) as c:
                chunk(c)

            block_reg = sp.alloc_register("block_reg")
            left_reg = sp.alloc_register("left_reg")
            turn_reg = sp.alloc_register("turn_reg")
            sp.reg_mov(block_reg, 0)
            sp.reg_mov(left_reg, NC)
            sp.reg_mov(turn_reg, 0)

            def load_next(m, u):
                sp.wait_ge(lo_ready, 2 * (NA - NC + m - RAW + 1))
                sp.dma_start(raw[:, u, :], row(adj, sp.snap(block_reg))).then_inc(raw_landed[u], 16)
                sp.reg_mov(block_reg, sp.snap(block_reg) + 1)
                sp.reg_mov(left_reg, sp.snap(left_reg) - 1)
                with sp.If(sp.snap(left_reg) == 0):
                    turn = sp.snap(turn_reg) + 1
                    sp.reg_mov(turn_reg, turn)
                    r = row_of(sp, turn)
                    sp.reg_mov(block_reg, NC * r)
                    sp.reg_mov(left_reg, NC - r)

            for u in range(RAW):
                load_next(u, u)
            store_x2(NC - 1)
            store_part(NC - 1)
            sp.wait_ge(adj_used, 2 * NA)
            sp.dma_start(w_raw[:, :, :], weights).then_inc(w_landed, 16)
            with sp.Fori(1, NB // RAW) as m4:
                for u in range(RAW):
                    load_next(RAW * m4 + u, u)

        @block.gpsimd
        def _(pool):
            pool.memset(power[:, :], -0.5).then_inc(power_set, 1)
            pool.memset(epsilon[:, :], EPS).then_inc(power_set, 1)
            pool.memset(tenth[:, :], ALPHA).then_inc(power_set, 1)

            def inverse_deviation(n, b):
                pool.wait_ge(moments_ready, n + 1)
                pool.tensor_tensor(var_eps[:, b, :], moments[:, b, :, 1], epsilon[:, :], ALU.add).then_inc(eps_added, 1)
                pool.wait_ge(eps_added, n + 1)
                pool.tensor_tensor(rstd[:, b, :], var_eps[:, b, :], power[:, :], ALU.pow).then_inc(rstd_ready, 1)

            def mix(c):
                if not isinstance(c, int):
                    pool.wait_ge(x2_ready, c)
                pool.wait_ge(cols_landed, 32 * (c + 1))
                pool.tensor_tensor(x_mix[:, :], hc_in[:, :], tenth[:, 0:1].to_broadcast([P, CH]), ALU.mult)\
                    .then_inc(mix_half, 1)
                pool.wait_ge(mix_half, c + 1)
                pool.tensor_tensor(x_mix[:, :], x_mix[:, :], xc_in[:, :], ALU.add).then_inc(mix_ready, 1)

            pool.wait_ge(power_set, 3)
            for q in range(NC):
                inverse_deviation(q, q % 2)
            mix(0)
            with pool.Fori(1, NC) as c:
                inverse_deviation(NC + c - 1, 0)
                mix(c)
            inverse_deviation(2 * NC - 1, 0)

            pool.wait_ge(adj_used, 2 * NA)
            pool.memset(part_in[:, :], 0.0).then_inc(part_landed, 16)
            pool.memset(result[:, :], 0.0).then_inc(out_stored, 16)
            pool.wait_ge(h_ready, 2 * NC)

            def sum_state(k):
                r = row_of(pool, k)
                hi = group(h2_hi, r).bitcast(FP32)
                lo = group(h2_lo, r).bitcast(FP32)
                if not isinstance(k, int) or k:
                    pool.wait_ge(state_turned, k)
                pool.tensor_tensor(h2_sum[:, :], hi, lo, ALU.add).then_inc(sum_ready, 1)

            def add_x2(k):
                pool.wait_ge(x2_landed, 16 * (k + 1))
                pool.wait_ge(out_stored, 16 * (k + 1))
                pool.wait_ge(gru_ready, k + 1)
                pool.tensor_tensor(result[:, :], gru[:, :], x2_in[:, :], ALU.add).then_inc(result_ready, 1)

            sum_state(0)
            sum_state(1)
            with pool.Fori(2, NC) as k:
                sum_state(k)
                add_x2(k - 2)
            add_x2(NC - 2)
            add_x2(NC - 1)

        @block.scalar
        def _(act):
            act.preload_act_table(ACT.Sigmoid)

            def hi_part(g, slot, turn):
                act.wait_ge(raw_landed[slot], 16 * turn)
                for h in range(2):
                    if not isinstance(g, int) or g >= NC + SPL:
                        act.wait_ge(adj_used, 2 * (g - SPL) + h + 1)
                    half = slice(h * HALF, (h + 1) * HALF)
                    act.activation(adj_hi[:, slot % SPL, half], raw[:, slot, half], ACT.Copy).then_inc(hi_ready, 1)

            def h1_hi_part(q):
                act.wait_ge(normed_ready, q + 1)
                if q >= 2:
                    act.wait_ge(adj_used, 2 * (q - 1))
                    act.wait_ge(h_ready, q - 1)
                act.activation(h1_now[:, q % 2, :], normed[:, :], ACT.Relu).then_inc(h1_now_ready, 1)
                act.wait_ge(h1_now_ready, q + 1)
                act.activation(h1_hi[:, q, :], h1_now[:, q % 2, :], ACT.Copy).then_inc(h_hi_ready, 1)

            def h_hi(n, table, k):
                act.wait_ge(normed_ready, n + 1)
                to = table[:, k, :] if isinstance(k, int) else \
                    table[:, bass.ds(k, 1), :].rearrange("p o n -> p (o n)")
                act.activation(to, normed[:, :], ACT.Relu).then_inc(h_hi_ready, 1)

            def part_evac(k):
                act.wait_ge(adj_used, 2 * NC * (k + 1))
                if not isinstance(k, int) or k > 1:
                    act.wait_ge(part_stored, 16 * (k - 1))
                act.activation(part_out[:, :], acc2[:, :], ACT.Copy).then_inc(part_ready, 1)

            for q in range(NC):
                h1_hi_part(q)

            def chunk(c):
                for q in range(NC):
                    hi_part(NC * c + q, q % RAW, (NC // RAW) * c + q // RAW + 1)
                    if q == 0:
                        if isinstance(c, int):
                            if c >= 2:
                                part_evac(c - 1)
                        else:
                            part_evac(c - 1)
                    if q == (1 if isinstance(c, int) else 3):
                        h_hi(NC + c - 1, h2_hi, c - 1)

            chunk(1)
            chunk(2)
            with act.Fori(3, NC) as c:
                chunk(c)
            part_evac(NC - 1)
            h_hi(2 * NC - 1, h2_hi, NC - 1)

            act.wait_ge(x2_stored, 16 * NC)
            act.wait_ge(part_stored, 16 * (NC - 1))
            act.wait_ge(w_landed, 16)
            act.activation(w_hi[:, :, :], w_raw[:, :, :], ACT.Copy).then_inc(w_hi_ready, 1)

            def load_part(k):
                r = row_of(act, k)
                act.dma_start(part_in[:, :], row(part_spill, r)).then_inc(part_landed, 16)

            def load_x2(k):
                r = row_of(act, k)
                act.dma_start(x2_in[:, :], row(x2_spill, r)).then_inc(x2_landed, 16)

            def store_result(k):
                r = row_of(act, k)
                act.wait_ge(result_ready, k + 1)
                act.dma_start(row(out, r), result[:, :]).then_inc(out_stored, 16)

            def agg_part(k):
                act.wait_ge(agg_out, k + 1)
                act.activation(agg_hi[:, :], agg[:, :], ACT.Copy).then_inc(agg_hi_ready, 1)

            def msg_part(k):
                act.wait_ge(msg_done, k + 1)
                act.activation(msg[:, :], acc2[:, :], ACT.Relu, bias=bias[:, MSG:MSG + 1]).then_inc(msg_out, 1)
                act.wait_ge(msg_out, k + 1)
                act.activation(msg_hi[:, :], msg[:, :], ACT.Copy).then_inc(msg_hi_ready, 1)

            def sigmoids(k):
                act.wait_ge(gates_done, k + 1)
                act.activation(reset[:, :], g_r[:, :], ACT.Sigmoid, bias=gate_bias[:, 0:1]).then_inc(reset_ready, 1)
                act.activation(update[:, :], g_z[:, :], ACT.Sigmoid, bias=gate_bias[:, 1:2]).then_inc(update_ready, 1)

            def new_state(k):
                act.wait_ge(pre_ready, k + 1)
                act.activation(new[:, :], pre_b[:, :], ACT.Tanh, bias=bias[:, I_N:I_N + 1]).then_inc(new_ready, 1)
                act.wait_ge(diff_ready, k + 1)
                act.activation(act_carrier[:, :], tenth[:, :], ACT.Copy)

            def state_part(k):
                act.wait_ge(state_turned, k + 1)
                act.activation(state[:, :], turned[:, :], ACT.Copy).then_inc(state_out, 1)
                act.activation(state_hi[:, :], turned[:, :], ACT.Copy).then_inc(state_hi_ready, 1)

            stored = act.alloc_register("act_stored")
            act.reg_mov(stored, 0)

            def first(last, before, m):
                with act.If(act.snap(last) >= 1):
                    msg_part(act.snap(before))
                agg_part(act.snap(last))
                load_part(act.snap(last) + 1)

            def second(last, before):
                with act.If(act.snap(last) >= 2):
                    store_result(act.snap(stored))
                    act.reg_mov(stored, act.snap(stored) + 1)
                with act.If(act.snap(last) >= 1):
                    load_x2(act.snap(before))
                    sigmoids(act.snap(before))

            def third(last, before):
                with act.If(act.snap(last) >= 1):
                    new_state(act.snap(before))
                state_part(act.snap(last))

            rows_of_pass_b(act, "act", lambda m, u: hi_part(NA + m, u, (NA + m - u) // RAW + 1), first, second, third)
            msg_part(NC - 2)
            agg_part(NC - 1)
            store_result(NC - 3)
            load_x2(NC - 2)
            sigmoids(NC - 2)
            new_state(NC - 2)
            state_part(NC - 1)
            msg_part(NC - 1)
            store_result(NC - 2)
            load_x2(NC - 1)
            sigmoids(NC - 1)
            new_state(NC - 1)
            store_result(NC - 1)
            act.wait_ge(out_stored, 16 * (NC + 1))

        @block.vector
        def _(dve):
            def lo_part(g, slot):
                for h in range(2):
                    if isinstance(g, int) and g == NC + SPL - 1 and h == 1:
                        dve.wait_ge(adj_used, 2 * NC)
                        dve.wait_ge(h_ready, NC)
                    dve.wait_ge(hi_ready, 2 * (g - NC) + h + 1)
                    half = slice(h * HALF, (h + 1) * HALF)
                    dve.tensor_tensor(adj_lo[:, slot % SPL, half], raw[:, slot, half],
                                      adj_hi[:, slot % SPL, half].bitcast(FP32), ALU.subtract).then_inc(lo_ready, 1)

            def statistics(n, rows, b):
                for t in range(JT):
                    last = dve.bn_stats(parts[:, b, t, :], rows[:, t * P:(t + 1) * P])
                last.then_inc(parts_ready, 1)
                dve.wait_ge(parts_ready, n + 1)
                dve.memset(carrier[:, :], 0.0)
                for t in range(JT):
                    last = dve.bn_aggr(moments[:, b, t, :], parts[:, b, t, :])
                last.then_inc(moments_ready, 1)

            def normalise(n, rows, b):
                if isinstance(n, int) and 0 < n < NC:
                    dve.wait_ge(h1_now_ready, n)
                elif not isinstance(n, int) or n:
                    dve.wait_ge(h_ready, n)
                dve.wait_ge(rstd_ready, n + 1)
                for t in range(JT):
                    last = dve.tensor_scalar(normed[:, t * P:(t + 1) * P], rows[:, t * P:(t + 1) * P],
                                             moments[:, b, t, 0:1], rstd[:, b, t:t + 1], ALU.subtract, ALU.mult)
                last.then_inc(normed_ready, 1)

            def h_lo(n, hi_table, lo_table, k):
                dve.wait_ge(h_hi_ready, n + 1)
                if isinstance(k, int):
                    hi, lo = hi_table[:, k, :], lo_table[:, k, :]
                else:
                    hi = hi_table[:, bass.ds(k, 1), :].rearrange("p o n -> p (o n)")
                    lo = lo_table[:, bass.ds(k, 1), :].rearrange("p o n -> p (o n)")
                dve.scalar_tensor_tensor(lo, normed[:, :], 0.0, hi.bitcast(FP32), ALU.max, ALU.subtract)\
                    .then_inc(h_ready, 1)

            def statistics_x(q):
                dve.wait_ge(x_landed[q % XS], 16 * (q // XS + 1))
                statistics(q, x_in[:, q, :], q % 2)

            def h1_lo_part(q):
                dve.wait_ge(h_hi_ready, q + 1)
                dve.tensor_tensor(h1_lo[:, q, :], h1_now[:, q % 2, :], h1_hi[:, q, :].bitcast(FP32), ALU.subtract)\
                    .then_inc(h_ready, 1)

            statistics_x(0)
            statistics_x(1)
            normalise(0, x_in[:, 0, :], 0)
            for q in range(NC):
                if q + 1 < NC:
                    normalise(q + 1, x_in[:, q + 1, :], (q + 1) % 2)
                if q + 2 < NC:
                    statistics_x(q + 2)
                h1_lo_part(q)

            def x2_evac(k):
                dve.wait_ge(adj_used, 2 * NC * (k + 1))
                dve.wait_ge(mix_ready, k + 1)
                if not isinstance(k, int) or k:
                    dve.wait_ge(x2_stored, 16 * k)
                src = acc[:, CH * (k % 2):CH * (k % 2) + CH] if isinstance(k, int) else \
                    acc[:, bass.ds(CH * (k % 2), CH)]
                dve.scalar_tensor_tensor(x2[:, :], src, 1.0 - ALPHA, x_mix[:, :], ALU.mult, ALU.add)\
                    .then_inc(x2_ready, 1)

            def x2_statistics(k):
                dve.wait_ge(x2_turned, k + 1)
                statistics(NC + k, turned[:, :], 0)

            def chunk(c):
                early = isinstance(c, int)
                for q in range(NC):
                    lo_part(NC * c + q, q % RAW)
                    if q == 0:
                        x2_evac(c - 1)
                    if q == 1:
                        x2_statistics(c - 1)
                    if q == (1 if early else 2):
                        normalise(NC + c - 1, turned[:, :], 0)
                    if q == (1 if early else 3):
                        h_lo(NC + c - 1, h2_hi, h2_lo, c - 1)

            chunk(1)
            chunk(2)
            with dve.Fori(3, NC) as c:
                chunk(c)
            x2_evac(NC - 1)
            x2_statistics(NC - 1)
            normalise(2 * NC - 1, turned[:, :], 0)
            h_lo(2 * NC - 1, h2_hi, h2_lo, NC - 1)

            dve.wait_ge(const_landed, 32)
            dve.tensor_tensor(gate_bias[:, :], bias[:, I_R:I_Z + 1], bias[:, H_R:H_Z + 1], ALU.add)\
                .then_inc(bias_ready, 1)
            dve.wait_ge(w_hi_ready, 1)
            dve.tensor_tensor(w_lo[:, :, :], w_raw[:, :, :], w_hi[:, :, :].bitcast(FP32), ALU.subtract)\
                .then_inc(w_ready, 1)

            def agg_evac(k, blocks_done):
                dve.wait_ge(adj_used, 2 * blocks_done)
                if isinstance(k, int):
                    src = acc[:, CH * (k % 2):CH * (k % 2) + CH]
                else:
                    src = acc[:, bass.ds(CH * (k % 2), CH)]
                dve.wait_ge(part_landed, 16 * (k + 1))
                dve.tensor_tensor(agg[:, :], src, part_in[:, :], ALU.add).then_inc(agg_out, 1)
                dve.wait_ge(agg_hi_ready, k + 1)
                dve.tensor_tensor(agg_lo[:, :], agg[:, :], agg_hi[:, :].bitcast(FP32), ALU.subtract)\
                    .then_inc(agg_ready, 1)

            def msg_split(k):
                dve.wait_ge(msg_hi_ready, k + 1)
                dve.tensor_tensor(msg_lo[:, :], msg[:, :], msg_hi[:, :].bitcast(FP32), ALU.subtract)\
                    .then_inc(msg_ready, 1)

            def new_input(k):
                dve.wait_ge(reset_ready, k + 1)
                dve.scalar_tensor_tensor(pre_a[:, :], g_hn[:, :], bias[:, H_N:H_N + 1], reset[:, :],
                                         ALU.add, ALU.mult).then_inc(pre_a_ready, 1)
                dve.wait_ge(pre_a_ready, k + 1)
                dve.tensor_tensor(pre_b[:, :], pre_a[:, :], g_in[:, :], ALU.add).then_inc(pre_ready, 1)

            def combine(k):
                dve.wait_ge(new_ready, k + 1)
                dve.tensor_tensor(diff[:, :], state[:, :], new[:, :], ALU.subtract).then_inc(diff_ready, 1)
                dve.wait_ge(diff_ready, k + 1)
                dve.wait_ge(update_ready, k + 1)
                dve.tensor_tensor(mixed[:, :], diff[:, :], update[:, :], ALU.mult).then_inc(mixed_ready, 1)
                dve.wait_ge(mixed_ready, k + 1)
                dve.tensor_tensor(gru[:, :], mixed[:, :], new[:, :], ALU.add).then_inc(gru_ready, 1)

            def state_split(k):
                dve.wait_ge(state_hi_ready, k + 1)
                dve.tensor_tensor(state_lo[:, :], state[:, :], state_hi[:, :].bitcast(FP32), ALU.subtract)\
                    .then_inc(state_ready, 1)

            def first(last, before, m):
                with dve.If(dve.snap(last) >= 1):
                    msg_split(dve.snap(before))
                agg_evac(dve.snap(last), NA + m)

            def second(last, before):
                with dve.If(dve.snap(last) >= 1):
                    new_input(dve.snap(before))

            def third(last, before):
                with dve.If(dve.snap(last) >= 1):
                    combine(dve.snap(before))
                state_split(dve.snap(last))

            rows_of_pass_b(dve, "dve", lambda m, u: lo_part(NA + m, u), first, second, third)
            msg_split(NC - 2)
            agg_evac(NC - 1, NA + NB)
            new_input(NC - 2)
            combine(NC - 2)
            state_split(NC - 1)
            msg_split(NC - 1)
            new_input(NC - 1)
            combine(NC - 1)

        @block.tensor
        def _(pe):
            def product(to, w_hi, w_lo, m_hi, m_lo, start):
                pe.matmul(to, w_hi, m_hi, start=start, stop=False, skip_group_check=True)
                pe.matmul(to, w_lo, m_hi, start=False, stop=False, skip_group_check=True)
                return pe.matmul(to, w_hi, m_lo, start=False, stop=False, skip_group_check=True)

            def aggregate(to, hi_table, lo_table, q, h, moving, start):
                for t in range(h * HT, (h + 1) * HT):
                    tile = slice(t * P, (t + 1) * P)
                    last = product(to, hi_table[:, q, tile], lo_table[:, q, tile], *moving(t), start and t == 0)
                return last

            def static_slot(slot):
                return lambda t: (adj_hi[:, slot, t * CH:(t + 1) * CH], adj_lo[:, slot, t * CH:(t + 1) * CH])

            def turn(src, ready, count, done):
                pe.wait_ge(ready, count)
                for t in range(JT):
                    last = pe.transpose(turned[:, t * P:(t + 1) * P], src[:, t * P:(t + 1) * P], ident[:, :])
                last.then_inc(done, 1)

            for q in range(NC):
                pe.wait_ge(h1_now_ready, q + 1)
                pe.wait_ge(raw_landed[q % RAW], 16 * (q // RAW + 1))
                for t in range(JT):
                    last = pe.matmul(acc[:, 0:CH], h1_now[:, q % 2, t * P:(t + 1) * P],
                                     raw[:, q % RAW, t * CH:(t + 1) * CH],
                                     start=q == 0 and t == 0, stop=False, skip_group_check=True)
                    if t % HT == HT - 1:
                        last.then_inc(adj_used, 1)
            pe.wait_ge(h_ready, NC)

            pe.wait_ge(const_landed, 32)
            with pe.Fori(1, NC) as c:
                bank1 = pe.snap(CH * (c % 2))
                def layer1(q, h):
                    return aggregate(acc[:, bass.ds(bank1, CH)], h1_hi, h1_lo, q, h, static_slot(q % SPL), q == 0)

                def layer2(q, h):
                    return aggregate(acc2[:, :], h2_hi, h2_lo, q, h, static_slot(q % SPL), q == 0)

                for h in range(2):
                    pe.wait_ge(lo_ready, 2 * NC * (c - 1) + h + 1)
                    layer1(0, h)
                turn(x2, x2_ready, c, x2_turned)
                with pe.If(c >= 2):
                    pe.wait_ge(part_ready, c - 1)
                pe.wait_ge(h_ready, NC + 1)
                for h in range(2):
                    layer2(0, h).then_inc(adj_used, 1)
                for q in range(1, NC):
                    for h in range(2):
                        pe.wait_ge(lo_ready, 2 * (NC * (c - 1) + q) + h + 1)
                        with pe.If(c > q):
                            if not h:
                                pe.wait_ge(h_ready, NC + q + 1)
                            layer2(q, h)
                        layer1(q, h).then_inc(adj_used, 1)
            turn(x2, x2_ready, NC, x2_turned)

            def gates(k):
                pe.wait_ge(state_ready, k + 1)
                for to, w in ((g_r, H_R), (g_z, H_Z), (g_hn, H_N)):
                    product(to[:, :], w_hi[:, w, :], w_lo[:, w, :], state_hi[:, :], state_lo[:, :], True)
                pe.wait_ge(msg_ready, k + 1)
                for to, w in ((g_r, I_R), (g_z, I_Z), (g_in, I_N)):
                    last = product(to[:, :], w_hi[:, w, :], w_lo[:, w, :], msg_hi[:, :], msg_lo[:, :], w == I_N)
                last.then_inc(gates_done, 1)

            def message(k):
                pe.wait_ge(agg_ready, k + 1)
                product(acc2[:, :], w_hi[:, MSG, :], w_lo[:, MSG, :], agg_hi[:, :], agg_lo[:, :], True)\
                    .then_inc(msg_done, 1)

            def turn_state(k):
                turn(h2_sum, sum_ready, k + 1, state_turned)

            pe.wait_ge(part_ready, NC - 1)
            done_reg = pe.alloc_register("pe_done")
            last_reg = pe.alloc_register("pe_last")
            before_reg = pe.alloc_register("pe_before")
            pe.reg_mov(done_reg, 0)
            pe.reg_mov(last_reg, 0)
            pe.reg_mov(before_reg, 0)
            with pe.Fori(0, NC) as turn_no:
                r = row_of(pe, turn_no)
                done = pe.snap(done_reg)
                acc_at = pe.snap(CH * (turn_no % 2))
                slots = [pe.snap(GW * ((done // 2 + i) % 2)) for i in range(2)]

                def block_of(q):
                    j = NC - 1 - q
                    pe.wait_ge(h_ready, NC + q + 1)
                    hi, lo = (a[:, :, :].rearrange("p s n -> p (s n)") for a in (adj_hi, adj_lo))
                    at = slots[j % 2]
                    for h in range(2):
                        pe.reg_mov(done_reg, pe.snap(done_reg) + 1)
                        pe.wait_ge(lo_ready, 2 * (NA - NC) + pe.snap(done_reg))
                        aggregate(acc[:, bass.ds(acc_at, CH)], h2_hi, h2_lo, q, h,
                                  lambda t: (hi[:, bass.ds(at + t * CH, CH)], lo[:, bass.ds(at + t * CH, CH)]), j == 0)\
                            .then_inc(adj_used, 1)

                block_of(NC - 1)
                with pe.If(turn_no >= 1):
                    with pe.If(turn_no >= 2):
                        gates(pe.snap(before_reg))
                    pe.wait_ge(w_ready, 1)
                    message(pe.snap(last_reg))
                    turn_state(pe.snap(last_reg))
                for q in range(NC - 2, -1, -1):
                    with pe.If(r <= q):
                        block_of(q)
                pe.reg_mov(before_reg, pe.snap(last_reg))
                pe.reg_mov(last_reg, turn_no)
            gates(NC - 2)
            message(NC - 1)
            turn_state(NC - 1)
            gates(NC - 1)


def kernel(x, adj, L0_gnn_h, L1_gnn_W_msg, L1_gnn_b_msg, L1_gnn_W_ih, L1_gnn_W_hh, L1_gnn_b_ih, L1_gnn_b_hh):
    import numpy as np
    import concourse.bacc as bacc
    from concourse.bass_utils import run_bass_kernel_spmd

    a = np.asarray
    blocks = a(adj).reshape(NC, CH, NC, JT, P).transpose(0, 2, 4, 3, 1)[:, ::-1].reshape(NA, P, GW)
    arrays = {
        "adj_in": blocks,
        "x_rows_in": a(x).reshape(NC, JT, P, P).transpose(0, 2, 1, 3).reshape(NC, P, HW),
        "x_cols_in": a(x).reshape(NC, CH, P).transpose(0, 2, 1),
        "h_cols_in": a(L0_gnn_h).reshape(NC, CH, P).transpose(0, 2, 1),
        "weights_in": np.concatenate([a(L1_gnn_W_msg), a(L1_gnn_W_ih), a(L1_gnn_W_hh)], 0).reshape(7, P, P).transpose(2, 0, 1),
        "biases_in": np.concatenate([a(L1_gnn_b_msg), a(L1_gnn_b_ih), a(L1_gnn_b_hh)], 0).reshape(7, P).transpose(1, 0),
        "identity_in": np.eye(P, dtype=np.float32),
    }
    arrays = {name: np.ascontiguousarray(v) for name, v in arrays.items()}
    nc = bacc.Bacc("TRN2", target_bir_lowering=False, num_devices=1)
    args = [nc.dram_tensor(name, v.shape, FP32, kind="ExternalInput").ap() for name, v in arrays.items()]
    out = nc.dram_tensor("out_cols", (NC, P, CH), FP32, kind="ExternalOutput").ap()
    gnn_program(nc, *args, out)
    r = run_bass_kernel_spmd(nc, [arrays], core_ids=[0])
    return np.ascontiguousarray(a(r.results[0]["out_cols"]).transpose(0, 2, 1).reshape(N, P))
```

```python
from contextlib import ExitStack

import concourse.bass as bass
from concourse import mybir

FP32 = mybir.dt.float32
FP32R = mybir.dt.float32r
ALU = mybir.AluOpType
ACT = mybir.ActivationFunctionType

P = 128
N = 8192
CH = 512
JT = 4
NC = N // CH
GW = JT * CH
RAW = 4
SPL = 2
ROW_RAW = 6
ROW_SPL = 3
XS = 8
HT = JT // 2
HALF = HT * CH
NH = 2 * SPL
HW = JT * P
NA = NC * NC
HELD = NC - 5
NB = NC * (NC + 1) // 2 - HELD
EARLY = 3
ALPHA = 0.1
EPS = 1e-5
MSG, I_R, I_Z, I_N, H_R, H_Z, H_N = range(7)


def gnn_program(nc, adj, x_rows, x_cols, h_cols, weights, biases, identity, out):
    x2_spill = nc.dram_tensor("x2_spill", (NC, P, CH), FP32).ap()
    part_spill = nc.dram_tensor("part_spill", (NC, P, CH), FP32).ap()
    ctx = ExitStack()
    with ctx:
        at = [-(-nc.sbuf_base // 64) * 64]

        def place(name, shape, dtype=FP32, offset=None):
            size = 4
            for n in shape[1:]:
                size *= n
            if offset is None:
                offset, at[0] = at[0], at[0] + -(-size // 64) * 64
            return nc.alloc_sbuf_tensor_at(name, shape, dtype, offset=offset)

        h1_at = at[0]
        h1_hi = place("h1_hi", [P, NC, HW], FP32R)
        h1_lo = place("h1_lo", [P, NC, HW], FP32R)
        raw = place("raw", [P, RAW, GW])
        power = place("power", [P, JT])
        epsilon = place("epsilon", [P, JT])
        carrier = place("carrier", [P, 1])
        act_carrier = place("act_carrier", [P, 1])
        bias = place("bias", [P, 7])
        gate_bias = place("gate_bias", [P, 2])
        ident = place("ident", [P, P])
        held = GW // HW
        assert HELD + 1 <= NC - held
        h2_hi = place("h2_hi", [P, NC, HW], FP32R)
        split_hi = place("split_hi", [P, (SPL + 1) * GW], FP32R, offset=at[0] - 4 * GW)
        pass_b_hi_at = at[0]
        at[0] += 4 * SPL * GW
        pass_b_hi_end = h2_lo_at = at[0]
        h2_lo = place("h2_lo", [P, NC, HW], FP32R)
        x_in = place("x_in", [P, NC, HW], offset=h2_lo_at)
        split_lo = place("split_lo", [P, (SPL + 1) * GW], FP32R, offset=at[0] - 4 * GW)
        pass_b_lo_at = at[0]
        at[0] += 4 * SPL * GW
        h1_now = place("h1_now", [P, 2, HW], offset=at[0] - 4 * 2 * HW)
        parts = place("parts", [P, 2, JT, 6])
        moments = place("moments", [P, 2, JT, 2])
        var_eps = place("var_eps", [P, 2, JT])
        rstd = place("rstd", [P, 2, JT])
        xc_in = place("xc_in", [P, CH])
        hc_in = place("hc_in", [P, CH])
        x_mix = place("x_mix", [P, CH])
        x2 = place("x2", [P, CH])
        normed = place("normed", [P, HW])
        part_out = place("part_out", [P, CH])
        assert at[0] <= nc.sbuf_usable_end
        raw_more = place("raw_more", [P, ROW_RAW - RAW, GW], offset=h1_at)
        row_hi = place("row_hi", [P, ROW_SPL, GW], FP32R, offset=h1_at + 4 * GW * (ROW_RAW - RAW))
        row_lo = place("row_lo", [P, ROW_SPL, GW], FP32R, offset=h1_at + 4 * GW * (ROW_RAW - RAW + ROW_SPL))
        assert ROW_RAW - RAW + 2 * ROW_SPL <= 2 * NC * HW // GW
        at[0] = pass_b_hi_at
        w_hi = place("w_hi", [P, 7, P], FP32R)
        w_lo = place("w_lo", [P, 7, P], FP32R)
        w_raw = place("w_raw", [P, 7, P], offset=at[0])
        state = place("state", [P, 2 * CH])
        reset = place("reset", [P, CH])
        update = place("update", [P, CH])
        assert at[0] <= pass_b_hi_end
        at[0] = pass_b_lo_at
        part_in = place("part_in", [P, CH])
        agg = place("agg", [P, CH])
        agg_hi = place("agg_hi", [P, CH], FP32R)
        agg_lo = place("agg_lo", [P, CH], FP32R)
        msg = place("msg", [P, CH])
        msg_hi = place("msg_hi", [P, CH], FP32R)
        msg_lo = place("msg_lo", [P, CH], FP32R)
        h2_sum = place("h2_sum", [P, HW])
        state_hi = place("state_hi", [P, CH], FP32R)
        state_lo = place("state_lo", [P, CH], FP32R)
        new = place("new", [P, CH])
        pre = place("pre", [P, CH])
        x2_in = place("x2_in", [P, CH])
        result = place("result", [P, CH])
        assert at[0] <= nc.sbuf_usable_end

        def bank(name, shape):
            return ctx.enter_context(nc.psum_tensor(name, shape, FP32))

        acc = bank("acc", [P, 2 * CH])
        acc2 = bank("acc2", [P, 2 * CH])
        msg_acc, g_hn = acc2[:, 0:CH], acc2[:, CH:2 * CH]
        turned = bank("turned", [P, CH])
        g_r = bank("g_r", [P, CH])
        g_z = bank("g_z", [P, CH])
        g_in = bank("g_in", [P, CH])

        def sem(name):
            return ctx.enter_context(nc.semaphore(name))

        x_landed = [sem(f"x_landed{i}") for i in range(XS)]
        raw_landed = [sem(f"raw_landed{i}") for i in range(ROW_RAW)]
        const_landed = sem("const_landed")
        cols_landed = sem("cols_landed")
        power_set = sem("power_set")
        hi_ready = sem("hi_ready")
        lo_ready = sem("lo_ready")
        adj_used = sem("adj_used")
        parts_ready = sem("parts_ready")
        moments_ready = sem("moments_ready")
        eps_added = sem("eps_added")
        rstd_ready = sem("rstd_ready")
        h1_now_ready = sem("h1_now_ready")
        normed_ready = sem("normed_ready")
        h_hi_ready = sem("h_hi_ready")
        h_ready = sem("h_ready")
        mix_ready = sem("mix_ready")
        x2_ready = sem("x2_ready")
        x2_stored = sem("x2_stored")
        x2_turned = sem("x2_turned")
        diag_used = sem("diag_used")
        part_ready = sem("part_ready")
        part_stored = sem("part_stored")
        w_landed = sem("w_landed")
        w_hi_ready = sem("w_hi_ready")
        w_ready = sem("w_ready")
        bias_ready = sem("bias_ready")
        part_landed = sem("part_landed")
        sum_ready = sem("sum_ready")
        state_turned = sem("state_turned")
        state_out = sem("state_out")
        state_hi_ready = sem("state_hi_ready")
        state_ready = sem("state_ready")
        agg_out = sem("agg_out")
        agg_hi_ready = sem("agg_hi_ready")
        agg_ready = sem("agg_ready")
        msg_done = sem("msg_done")
        msg_out = sem("msg_out")
        msg_hi_ready = sem("msg_hi_ready")
        msg_ready = sem("msg_ready")
        gates_done = sem("gates_done")
        reset_ready = sem("reset_ready")
        update_ready = sem("update_ready")
        pre_a_ready = sem("pre_a_ready")
        pre_ready = sem("pre_ready")
        new_ready = sem("new_ready")
        diff_ready = sem("diff_ready")
        mixed_ready = sem("mixed_ready")
        gru_ready = sem("gru_ready")
        x2_landed = sem("x2_landed")
        result_ready = sem("result_ready")
        out_stored = sem("out_stored")

        def row(t, k):
            return t[k] if isinstance(k, int) else t[bass.ds(k, 1)].rearrange("o p n -> (o p) n")

        def group(table, k):
            return table[:, k, :] if isinstance(k, int) else table[:, bass.ds(k, 1), :].rearrange("p o n -> p (o n)")

        def row_slot(slot):
            return raw[:, slot, :] if slot < RAW else raw_more[:, slot - RAW, :]

        def state_of(turn):
            at = CH * (turn % 2)
            return state[:, at:at + CH] if isinstance(turn, int) else state[:, bass.ds(at, CH)]

        def row_of(eng, turn):
            r = (turn // 2 + (turn % 2) * (NC - 1 - 2 * (turn // 2))) % NC
            return r if isinstance(turn, int) else eng.snap(r)

        def blocks_of(r):
            return NC - 1 - r + (r > HELD)

        def split_slot(eng, c, q):
            at = GW * (1 + q % SPL)
            if isinstance(c, int):
                return 0 if c == q <= HELD else at
            return at if q == 0 or q > HELD else eng.snap((c != q) * at)

        def rows_of_pass_b(eng, name, split, first, second, third):
            last = eng.alloc_register(name + "_last")
            before = eng.alloc_register(name + "_before")
            first_at = eng.alloc_register(name + "_first_at")
            second_at = eng.alloc_register(name + "_second_at")
            third_at = eng.alloc_register(name + "_third_at")
            for register, value in ((last, 0), (before, 0), (first_at, NC), (second_at, NB), (third_at, NB)):
                eng.reg_mov(register, value)
            first_blocks = NB % ROW_RAW
            with eng.Fori(0, NB // ROW_RAW) as rounds:
                for u in range(ROW_RAW):
                    m = ROW_RAW * rounds + first_blocks + u
                    split(m, (first_blocks + u) % ROW_RAW)
                    with eng.If(m == eng.snap(second_at)):
                        second(last, before)
                    with eng.If(m == eng.snap(third_at)):
                        third(last, before)
                        eng.reg_mov(before, eng.snap(last))
                        eng.reg_mov(last, eng.snap(last) + 1)
                    with eng.If(m == eng.snap(first_at)):
                        first(last, before, m)
                        blocks = eng.snap(blocks_of(row_of(eng, eng.snap(last) + 1)))
                        eng.reg_mov(second_at, m + 2 - (blocks < 2))
                        eng.reg_mov(third_at, m + 3 - (blocks < 2) - (blocks < 3))
                        eng.reg_mov(first_at, m + blocks)

        block = ctx.enter_context(nc.Block())

        @block.sync
        def _(sp):
            def load_x(q):
                sp.dma_start(x_in[:, q, :], x_rows[q]).then_inc(x_landed[q % XS], 16)

            def load_block(c, q):
                before = NC * c + q - RAW
                if isinstance(c, int):
                    if 0 <= before < NC:
                        sp.wait_ge(adj_used, 2 * (before + 1))
                    if before >= NC:
                        sp.wait_ge(lo_ready, 2 * (before - NC + 1))
                else:
                    sp.wait_ge(lo_ready, 2 * (before - NC + 1))
                sp.dma_start(raw[:, q % RAW, :], adj[NC * c + NC - 1 - q]).then_inc(raw_landed[q % RAW], 16)

            def load_cols(c):
                if not isinstance(c, int):
                    sp.wait_ge(mix_ready, c)
                sp.dma_start(xc_in[:, :], row(x_cols, c)).then_inc(cols_landed, 16)
                sp.dma_start(hc_in[:, :], row(h_cols, c)).then_inc(cols_landed, 16)

            def store_x2(k):
                sp.wait_ge(x2_ready, k + 1)
                sp.dma_start(row(x2_spill, k), x2[:, :]).then_inc(x2_stored, 16)

            def store_part(k):
                sp.wait_ge(part_ready, k + 2)
                sp.dma_start(row(part_spill, k), part_out[:, :]).then_inc(part_stored, 16)

            for q in range(4):
                load_x(q)
            for q in range(NC):
                load_block(0, q)
                if q + 4 < NC:
                    load_x(q + 4)
            load_cols(0)
            sp.dma_start(ident[:, :], identity).then_inc(const_landed, 16)
            sp.dma_start(bias[:, :], biases).then_inc(const_landed, 16)

            def chunk(c):
                for q in range(NC):
                    load_block(c, q)
                    if q == 6:
                        store_x2(c - 1)
                        if not isinstance(c, int):
                            store_part(c - 2)
                    if q == 8:
                        load_cols(c)

            chunk(1)
            with sp.Fori(2, NC) as c:
                chunk(c)

            first_blocks = [(m + 1) % NC for m in range(NC)]
            for turn in range(1, NC):
                r = row_of(sp, turn)
                first_blocks += [NC * r + i for i in range(blocks_of(r))]
            peeled = NC + (NB - NC) % ROW_RAW
            def load_first(m):
                if m < RAW:
                    sp.wait_ge(lo_ready, 2 * (NA - NC + m - RAW + 1))
                elif m >= ROW_RAW:
                    sp.wait_ge(lo_ready, 2 * (NA - NC + m - ROW_RAW + 1))
                slot = m % ROW_RAW
                sp.dma_start(row_slot(slot), adj[first_blocks[m]]).then_inc(raw_landed[slot], 16)

            for m in range(RAW):
                load_first(m)
                if m == 2:
                    store_part(NC - 2)
            store_x2(NC - 1)
            store_part(NC - 1)
            sp.wait_ge(adj_used, 2 * NA)
            for m in range(RAW, ROW_RAW):
                load_first(m)
            sp.dma_start(w_raw[:, :, :], weights).then_inc(w_landed, 16)
            for m in range(ROW_RAW, peeled):
                load_first(m)

            block_reg = sp.alloc_register("block_reg")
            left_reg = sp.alloc_register("left_reg")
            turn_reg = sp.alloc_register("turn_reg")
            assert NC + 1 <= peeled < NC + 1 + blocks_of(1)
            sp.reg_mov(block_reg, first_blocks[peeled])
            sp.reg_mov(left_reg, NC + 1 + blocks_of(1) - peeled)
            sp.reg_mov(turn_reg, 2)

            with sp.Fori(0, (NB - peeled) // ROW_RAW) as rounds:
                for u in range(ROW_RAW):
                    m = ROW_RAW * rounds + peeled + u
                    slot = (peeled + u) % ROW_RAW
                    sp.wait_ge(lo_ready, 2 * (NA - NC + m - ROW_RAW + 1))
                    sp.dma_start(row_slot(slot), row(adj, sp.snap(block_reg))).then_inc(raw_landed[slot], 16)
                    sp.reg_mov(block_reg, sp.snap(block_reg) + 1)
                    sp.reg_mov(left_reg, sp.snap(left_reg) - 1)
                    with sp.If(sp.snap(left_reg) == 0):
                        turn = sp.snap(turn_reg) + 1
                        sp.reg_mov(turn_reg, turn)
                        r = row_of(sp, turn)
                        sp.reg_mov(block_reg, NC * r)
                        sp.reg_mov(left_reg, blocks_of(r))

        @block.gpsimd
        def _(pool):
            pool.memset(power[:, :], -0.5).then_inc(power_set, 1)
            pool.memset(epsilon[:, :], EPS).then_inc(power_set, 1)
            pool.memset(part_out[:, :], 0.0).then_inc(part_ready, 2)

            def inverse_deviation(n, b):
                pool.wait_ge(moments_ready, n + 1)
                pool.tensor_tensor(var_eps[:, b, :], moments[:, b, :, 1], epsilon[:, :], ALU.add).then_inc(eps_added, 1)
                pool.wait_ge(eps_added, n + 1)
                pool.tensor_tensor(rstd[:, b, :], var_eps[:, b, :], power[:, :], ALU.pow).then_inc(rstd_ready, 1)

            pool.wait_ge(power_set, 2)
            for q in range(NC):
                inverse_deviation(q, q % 2)
            with pool.Fori(1, NC) as c:
                inverse_deviation(NC + c - 1, 0)
            inverse_deviation(2 * NC - 1, 0)

            pool.wait_ge(h_ready, 2 * NC)
            pool.wait_ge(adj_used, 2 * NA)
            pool.wait_ge(x2_stored, 16 * NC)
            pool.wait_ge(part_stored, 16 * NC)
            pool.memset(update[:, 0:1], 0.0).then_inc(diff_ready, 2)
            pool.memset(new[:, 0:1], 0.0).then_inc(gru_ready, 1)

            def sum_state(k):
                if not isinstance(k, int) or k:
                    pool.wait_ge(state_turned, k)
                r = row_of(pool, k)
                pool.tensor_tensor(h2_sum[:, :], group(h2_hi, r).bitcast(FP32), group(h2_lo, r).bitcast(FP32),
                                   ALU.add).then_inc(sum_ready, 1)

            def load_part(k):
                if not isinstance(k, int) or k:
                    pool.wait_ge(agg_out, k)
                pool.dma_start(part_in[:, :], row(part_spill, row_of(pool, k))).then_inc(part_landed, 16)

            def load_x2(k):
                if not isinstance(k, int) or k:
                    pool.wait_ge(result_ready, k)
                pool.dma_start(x2_in[:, :], row(x2_spill, row_of(pool, k))).then_inc(x2_landed, 16)

            def new_state(k):
                if not isinstance(k, int) or k:
                    pool.wait_ge(out_stored, 16 * k)
                pool.wait_ge(new_ready, k + 1)
                pool.tensor_tensor(result[:, :], state_of(k), new[:, :], ALU.subtract).then_inc(diff_ready, 1)
                pool.wait_ge(update_ready, k + 1)
                pool.wait_ge(diff_ready, k + 3)
                pool.tensor_tensor(result[:, :], result[:, :], update[:, :], ALU.mult).then_inc(mixed_ready, 1)
                pool.wait_ge(mixed_ready, k + 1)
                pool.tensor_tensor(result[:, :], result[:, :], new[:, :], ALU.add).then_inc(gru_ready, 1)
                pool.wait_ge(x2_landed, 16 * (k + 1))
                pool.wait_ge(gru_ready, k + 2)
                pool.tensor_tensor(result[:, :], result[:, :], x2_in[:, :], ALU.add).then_inc(result_ready, 1)

            def store_result(k):
                pool.wait_ge(result_ready, k + 1)
                pool.dma_start(row(out, row_of(pool, k)), result[:, :]).then_inc(out_stored, 16)

            sum_state(0)
            load_part(0)
            load_x2(0)
            load_part(1)
            sum_state(1)

            def turn(k):
                load_part(k)
                sum_state(k)
                new_state(k - 2)
                store_result(k - 2)
                load_x2(k - 1)

            turn(2)
            with pool.Fori(3, NC) as k:
                turn(k)
            new_state(NC - 2)
            store_result(NC - 2)
            load_x2(NC - 1)
            new_state(NC - 1)
            store_result(NC - 1)
            pool.wait_ge(out_stored, 16 * NC)

        @block.scalar
        def _(act):
            act.preload_act_table(ACT.Sigmoid)

            def hi_part(c, q):
                g, slot = NC * c + q, q % RAW
                if q <= HELD:
                    if not isinstance(c, int) and q > EARLY:
                        with act.If(c == q):
                            act.wait_ge(diag_used, q - 1)
                            act.activation(act_carrier[:, :], rstd[:, 0, 0:1], ACT.Copy)
                    elif isinstance(c, int) and c == q >= 2:
                        act.wait_ge(diag_used, q - 1)
                act.wait_ge(raw_landed[slot], 16 * ((NC // RAW) * c + q // RAW + 1))
                at = split_slot(act, c, q)
                for h in range(2):
                    if not isinstance(g, int) or g >= NC + SPL:
                        act.wait_ge(adj_used, 2 * (g - SPL) + h + 1)
                    act.activation(split_hi[:, bass.ds(at + h * HALF, HALF)],
                                   raw[:, slot, h * HALF:(h + 1) * HALF], ACT.Copy).then_inc(hi_ready, 1)

            def row_hi_part(m, slot):
                loads = (m - slot) // ROW_RAW + 1 + (NA // RAW if slot < RAW else 0)
                act.wait_ge(raw_landed[slot], 16 * loads)
                for h in range(2):
                    first_round = isinstance(m, int) and m < ROW_SPL
                    act.wait_ge(adj_used, 2 * NA if first_round else 2 * (NA + m - ROW_SPL) + h + 1)
                    half = slice(h * HALF, (h + 1) * HALF)
                    act.activation(row_hi[:, slot % ROW_SPL, half], row_slot(slot)[:, half], ACT.Copy)\
                        .then_inc(hi_ready, 1)

            def h1_hi_part(q):
                act.wait_ge(normed_ready, q + 1)
                if q >= 2:
                    act.wait_ge(adj_used, 2 * (q - 1))
                    act.wait_ge(h_ready, q - 1)
                act.activation(h1_now[:, q % 2, :], normed[:, :], ACT.Relu).then_inc(h1_now_ready, 1)
                act.wait_ge(h1_now_ready, q + 1)
                act.activation(h1_hi[:, q, :], h1_now[:, q % 2, :], ACT.Copy).then_inc(h_hi_ready, 1)

            def h_hi(n, table, k):
                act.wait_ge(normed_ready, n + 1)
                to = table[:, k, :] if isinstance(k, int) else \
                    table[:, bass.ds(k, 1), :].rearrange("p o n -> p (o n)")
                act.activation(to, normed[:, :], ACT.Relu).then_inc(h_hi_ready, 1)

            def part_evac(k):
                if isinstance(k, int) and k == NC - 1:
                    act.wait_ge(adj_used, 2 * NA)
                act.wait_ge(part_stored, 16 * k)
                src = acc2[:, CH * (k % 2):CH * (k % 2) + CH] if isinstance(k, int) else \
                    acc2[:, bass.ds(CH * (k % 2), CH)]
                act.activation(part_out[:, :], src, ACT.Copy).then_inc(part_ready, 1)

            for q in range(NC):
                h1_hi_part(q)

            def chunk(c):
                for q in range(NC):
                    hi_part(c, q)
                    if q == (1 if isinstance(c, int) else 3):
                        h_hi(NC + c - 1, h2_hi, c - 1)
                    if q == NC - 1 and not (isinstance(c, int) and c == 1):
                        part_evac(c - 1)

            for c in range(1, EARLY + 1):
                chunk(c)
            with act.Fori(EARLY + 1, NC) as c:
                chunk(c)
            part_evac(NC - 1)

            for m in range(NB % ROW_RAW):
                row_hi_part(m, m)
            h_hi(2 * NC - 1, h2_hi, NC - 1)
            act.wait_ge(w_landed, 16)
            act.activation(w_hi[:, :, :], w_raw[:, :, :], ACT.Copy).then_inc(w_hi_ready, 1)

            def msg_part(k):
                act.wait_ge(msg_done, k + 1)
                act.activation(msg[:, :], msg_acc, ACT.Relu, bias=bias[:, MSG:MSG + 1]).then_inc(msg_out, 1)
                act.wait_ge(msg_out, k + 1)
                act.activation(msg_hi[:, :], msg[:, :], ACT.Copy).then_inc(msg_hi_ready, 1)

            def sigmoids(k):
                act.wait_ge(gates_done, k + 1)
                act.activation(reset[:, :], g_r[:, :], ACT.Sigmoid, bias=gate_bias[:, 0:1]).then_inc(reset_ready, 1)
                act.wait_ge(gru_ready, k + 1)
                act.activation(update[:, :], g_z[:, :], ACT.Sigmoid, bias=gate_bias[:, 1:2]).then_inc(update_ready, 1)

            def new_state(k):
                act.wait_ge(pre_ready, k + 1)
                act.activation(new[:, :], pre[:, :], ACT.Tanh, bias=bias[:, I_N:I_N + 1]).then_inc(new_ready, 1)

            def state_part(k):
                act.wait_ge(state_turned, k + 1)
                act.wait_ge(diff_ready, k + 1)
                act.activation(state_of(k), turned[:, :], ACT.Copy).then_inc(state_out, 1)
                act.activation(state_hi[:, :], turned[:, :], ACT.Copy).then_inc(state_hi_ready, 1)

            def first(last, before, m):
                with act.If(act.snap(last) >= 1):
                    msg_part(act.snap(before))

            def second(last, before):
                with act.If(act.snap(last) >= 1):
                    sigmoids(act.snap(before))

            def third(last, before):
                with act.If(act.snap(last) >= 1):
                    new_state(act.snap(before))
                state_part(act.snap(last))

            rows_of_pass_b(act, "act", row_hi_part, first, second, third)
            msg_part(NC - 2)
            sigmoids(NC - 2)
            new_state(NC - 2)
            state_part(NC - 1)
            msg_part(NC - 1)
            sigmoids(NC - 1)
            new_state(NC - 1)

        @block.vector
        def _(dve):
            def lo_part(c, q):
                g, slot = NC * c + q, q % RAW
                at = split_slot(dve, c, q)
                for h in range(2):
                    if isinstance(c, int) and (c, q, h) == (1, SPL + 1, 1):
                        dve.wait_ge(adj_used, 2 * NC)
                        dve.wait_ge(h_ready, NC)
                    dve.wait_ge(hi_ready, 2 * (g - NC) + h + 1)
                    half = bass.ds(at + h * HALF, HALF)
                    dve.tensor_tensor(split_lo[:, half], raw[:, slot, h * HALF:(h + 1) * HALF],
                                      split_hi[:, half].bitcast(FP32), ALU.subtract).then_inc(lo_ready, 1)

            def row_lo_part(m, slot):
                for h in range(2):
                    dve.wait_ge(hi_ready, 2 * (NA - NC + m) + h + 1)
                    half = slice(h * HALF, (h + 1) * HALF)
                    dve.tensor_tensor(row_lo[:, slot % ROW_SPL, half], row_slot(slot)[:, half],
                                      row_hi[:, slot % ROW_SPL, half].bitcast(FP32), ALU.subtract)\
                        .then_inc(lo_ready, 1)

            def statistics(n, rows, b):
                for t in range(JT):
                    last = dve.bn_stats(parts[:, b, t, :], rows[:, t * P:(t + 1) * P])
                last.then_inc(parts_ready, 1)
                dve.wait_ge(parts_ready, n + 1)
                dve.memset(carrier[:, :], 0.0)
                for t in range(JT):
                    last = dve.bn_aggr(moments[:, b, t, :], parts[:, b, t, :])
                last.then_inc(moments_ready, 1)

            def normalise(n, rows, b):
                if isinstance(n, int) and 0 < n < NC:
                    dve.wait_ge(h1_now_ready, n)
                elif not isinstance(n, int) or n:
                    dve.wait_ge(h_ready, n)
                dve.wait_ge(rstd_ready, n + 1)
                for t in range(JT):
                    last = dve.tensor_scalar(normed[:, t * P:(t + 1) * P], rows[:, t * P:(t + 1) * P],
                                             moments[:, b, t, 0:1], rstd[:, b, t:t + 1], ALU.subtract, ALU.mult)
                last.then_inc(normed_ready, 1)

            def h_lo(n, hi_table, lo_table, k):
                dve.wait_ge(h_hi_ready, n + 1)
                if isinstance(k, int):
                    hi, lo = hi_table[:, k, :], lo_table[:, k, :]
                else:
                    hi = hi_table[:, bass.ds(k, 1), :].rearrange("p o n -> p (o n)")
                    lo = lo_table[:, bass.ds(k, 1), :].rearrange("p o n -> p (o n)")
                dve.scalar_tensor_tensor(lo, normed[:, :], 0.0, hi.bitcast(FP32), ALU.max, ALU.subtract)\
                    .then_inc(h_ready, 1)

            def statistics_x(q):
                dve.wait_ge(x_landed[q % XS], 16 * (q // XS + 1))
                statistics(q, x_in[:, q, :], q % 2)

            def h1_lo_part(q):
                dve.wait_ge(h_hi_ready, q + 1)
                dve.tensor_tensor(h1_lo[:, q, :], h1_now[:, q % 2, :], h1_hi[:, q, :].bitcast(FP32), ALU.subtract)\
                    .then_inc(h_ready, 1)

            statistics_x(0)
            statistics_x(1)
            normalise(0, x_in[:, 0, :], 0)
            for q in range(NC):
                if q + 1 < NC:
                    normalise(q + 1, x_in[:, q + 1, :], (q + 1) % 2)
                if q + 2 < NC:
                    statistics_x(q + 2)
                h1_lo_part(q)

            def mix(c):
                dve.wait_ge(cols_landed, 32 * (c + 1))
                if not isinstance(c, int) or c:
                    dve.wait_ge(x2_ready, c)
                dve.scalar_tensor_tensor(x_mix[:, :], hc_in[:, :], ALPHA, xc_in[:, :], ALU.mult, ALU.add)\
                    .then_inc(mix_ready, 1)

            mix(0)

            def x2_evac(k):
                dve.wait_ge(adj_used, 2 * NC * (k + 1))
                dve.wait_ge(mix_ready, k + 1)
                if not isinstance(k, int) or k:
                    dve.wait_ge(x2_stored, 16 * k)
                src = acc[:, CH * (k % 2):CH * (k % 2) + CH] if isinstance(k, int) else \
                    acc[:, bass.ds(CH * (k % 2), CH)]
                dve.scalar_tensor_tensor(x2[:, :], src, 1.0 - ALPHA, x_mix[:, :], ALU.mult, ALU.add)\
                    .then_inc(x2_ready, 1)

            def x2_statistics(k):
                dve.wait_ge(x2_turned, k + 1)
                statistics(NC + k, turned[:, :], 0)

            def chunk(c):
                early = isinstance(c, int)
                for q in range(NC):
                    lo_part(c, q)
                    if q == 0:
                        x2_evac(c - 1)
                    if q == 1:
                        x2_statistics(c - 1)
                    if q == (1 if early else 2):
                        normalise(NC + c - 1, turned[:, :], 0)
                    if q == (1 if early else 3):
                        h_lo(NC + c - 1, h2_hi, h2_lo, c - 1)
                    if q == NC - 4:
                        mix(c)

            for c in range(1, EARLY + 1):
                chunk(c)
            with dve.Fori(EARLY + 1, NC) as c:
                chunk(c)
            x2_evac(NC - 1)

            for m in range(NB % ROW_RAW):
                row_lo_part(m, m)
                if m == 1:
                    x2_statistics(NC - 1)
                if m == 2:
                    normalise(2 * NC - 1, turned[:, :], 0)
            h_lo(2 * NC - 1, h2_hi, h2_lo, NC - 1)
            dve.wait_ge(const_landed, 32)
            dve.tensor_tensor(gate_bias[:, :], bias[:, I_R:I_Z + 1], bias[:, H_R:H_Z + 1], ALU.add)\
                .then_inc(bias_ready, 1)
            dve.wait_ge(w_hi_ready, 1)
            dve.tensor_tensor(w_lo[:, :, :], w_raw[:, :, :], w_hi[:, :, :].bitcast(FP32), ALU.subtract)\
                .then_inc(w_ready, 1)

            def agg_evac(k, blocks_done):
                dve.wait_ge(adj_used, 2 * blocks_done)
                if isinstance(k, int):
                    src = acc[:, CH * (k % 2):CH * (k % 2) + CH]
                else:
                    src = acc[:, bass.ds(CH * (k % 2), CH)]
                dve.wait_ge(part_landed, 16 * (k + 1))
                dve.tensor_tensor(agg[:, :], src, part_in[:, :], ALU.add).then_inc(agg_out, 1)
                dve.wait_ge(agg_out, k + 1)
                dve.tensor_copy(agg_hi[:, :], agg[:, :]).then_inc(agg_hi_ready, 1)
                dve.wait_ge(agg_hi_ready, k + 1)
                dve.tensor_tensor(agg_lo[:, :], agg[:, :], agg_hi[:, :].bitcast(FP32), ALU.subtract)\
                    .then_inc(agg_ready, 1)

            def msg_split(k):
                dve.wait_ge(msg_hi_ready, k + 1)
                dve.tensor_tensor(msg_lo[:, :], msg[:, :], msg_hi[:, :].bitcast(FP32), ALU.subtract)\
                    .then_inc(msg_ready, 1)

            def new_input(k):
                dve.wait_ge(reset_ready, k + 1)
                dve.scalar_tensor_tensor(pre[:, :], g_hn, bias[:, H_N:H_N + 1], reset[:, :],
                                         ALU.add, ALU.mult).then_inc(pre_a_ready, 1)
                dve.wait_ge(pre_a_ready, k + 1)
                dve.tensor_tensor(pre[:, :], pre[:, :], g_in[:, :], ALU.add).then_inc(pre_ready, 1)

            def state_split(k):
                dve.wait_ge(state_hi_ready, k + 1)
                dve.tensor_tensor(state_lo[:, :], state_of(k), state_hi[:, :].bitcast(FP32), ALU.subtract)\
                    .then_inc(state_ready, 1)

            def first(last, before, m):
                with dve.If(dve.snap(last) >= 1):
                    msg_split(dve.snap(before))
                agg_evac(dve.snap(last), NA + m)

            def second(last, before):
                with dve.If(dve.snap(last) >= 1):
                    new_input(dve.snap(before))

            def third(last, before):
                state_split(dve.snap(last))

            rows_of_pass_b(dve, "dve", row_lo_part, first, second, third)
            msg_split(NC - 2)
            agg_evac(NC - 1, NA + NB)
            new_input(NC - 2)
            state_split(NC - 1)
            msg_split(NC - 1)
            new_input(NC - 1)

        @block.tensor
        def _(pe):
            def product(to, w_hi, w_lo, m_hi, m_lo, start):
                pe.matmul(to, w_hi, m_hi, start=start, stop=False, skip_group_check=True)
                pe.matmul(to, w_lo, m_hi, start=False, stop=False, skip_group_check=True)
                return pe.matmul(to, w_hi, m_lo, start=False, stop=False, skip_group_check=True)

            def aggregate(to, hi_table, lo_table, q, h, moving, start):
                for t in range(h * HT, (h + 1) * HT):
                    tile = slice(t * P, (t + 1) * P)
                    last = product(to, hi_table[:, q, tile], lo_table[:, q, tile], *moving(t), start and t == 0)
                return last

            def split_at(at):
                return lambda t: (split_hi[:, bass.ds(at + t * CH, CH)], split_lo[:, bass.ds(at + t * CH, CH)])

            def turn(src, ready, count, done):
                pe.wait_ge(ready, count)
                for t in range(JT):
                    last = pe.transpose(turned[:, t * P:(t + 1) * P], src[:, t * P:(t + 1) * P], ident[:, :])
                last.then_inc(done, 1)

            for q in range(NC):
                pe.wait_ge(h1_now_ready, q + 1)
                pe.wait_ge(raw_landed[q % RAW], 16 * (q // RAW + 1))
                for t in range(JT):
                    last = pe.matmul(acc[:, 0:CH], h1_now[:, q % 2, t * P:(t + 1) * P],
                                     raw[:, q % RAW, t * CH:(t + 1) * CH],
                                     start=q == 0 and t == 0, stop=False, skip_group_check=True)
                    if t % HT == HT - 1:
                        last.then_inc(adj_used, 1)
            pe.wait_ge(h_ready, NC)

            pe.wait_ge(const_landed, 32)
            with pe.Fori(1, NC) as c:
                bank1 = pe.snap(CH * (c % 2))
                def layer1(q, h):
                    return aggregate(acc[:, bass.ds(bank1, CH)], h1_hi, h1_lo, q, h, split_at(split_slot(pe, c, q)), q == 0)

                def layer2(q, h):
                    return aggregate(acc2[:, bass.ds(bank1, CH)], h2_hi, h2_lo, q, h, split_at(GW * (1 + q % SPL)), q == 0)

                def diagonal(q):
                    aggregate(acc2[:, CH * (q % 2):CH * (q % 2) + CH], h2_hi, h2_lo, q, 0, split_at(0), False)
                    aggregate(acc2[:, CH * (q % 2):CH * (q % 2) + CH], h2_hi, h2_lo, q, 1, split_at(0), False)\
                        .then_inc(diag_used, 1)

                for h in range(2):
                    pe.wait_ge(lo_ready, 2 * NC * (c - 1) + h + 1)
                    layer1(0, h)
                turn(x2, x2_ready, c, x2_turned)
                pe.wait_ge(part_ready, c)
                pe.wait_ge(h_ready, NC + 1)
                for h in range(2):
                    layer2(0, h).then_inc(adj_used, 1)
                for q in range(1, NC):
                    for h in range(2):
                        pe.wait_ge(lo_ready, 2 * (NC * (c - 1) + q) + h + 1)
                        with pe.If(c > q):
                            if not h:
                                pe.wait_ge(h_ready, NC + q + 1)
                                if 1 <= q <= HELD:
                                    with pe.If(c == q + 1):
                                        diagonal(q)
                            layer2(q, h)
                        layer1(q, h).then_inc(adj_used, 1)

            def gates(k):
                pe.wait_ge(state_ready, k + 1)
                for to, w in ((g_r, H_R), (g_z, H_Z), (g_hn, H_N)):
                    product(to[:, :], w_hi[:, w, :], w_lo[:, w, :], state_hi[:, :], state_lo[:, :], True)
                pe.wait_ge(msg_ready, k + 1)
                for to, w in ((g_r, I_R), (g_z, I_Z), (g_in, I_N)):
                    last = product(to[:, :], w_hi[:, w, :], w_lo[:, w, :], msg_hi[:, :], msg_lo[:, :], w == I_N)
                last.then_inc(gates_done, 1)

            def message(k):
                pe.wait_ge(agg_ready, k + 1)
                product(msg_acc, w_hi[:, MSG, :], w_lo[:, MSG, :], agg_hi[:, :], agg_lo[:, :], True)\
                    .then_inc(msg_done, 1)

            def turn_state(k):
                turn(h2_sum, sum_ready, k + 1, state_turned)

            hi_slots, lo_slots = (a[:, :, :].rearrange("p s n -> p (s n)") for a in (row_hi, row_lo))

            for m in range(NC):
                at = GW * (m % ROW_SPL)
                for h in range(2):
                    pe.wait_ge(lo_ready, 2 * (NA - NC + m) + h + 1)
                    if m == NC - 1 and h == 0:
                        pe.wait_ge(h_ready, 2 * NC)
                    aggregate(acc[:, 0:CH], h2_hi, h2_lo, (NC - 2 - m) % NC, h,
                              lambda t: (hi_slots[:, at + t * CH:at + t * CH + CH],
                                         lo_slots[:, at + t * CH:at + t * CH + CH]), m == 0).then_inc(adj_used, 1)
                if m == 0:
                    turn(x2, x2_ready, NC, x2_turned)
            pe.wait_ge(part_ready, NC + 1)

            done_reg = pe.alloc_register("pe_done")
            last_reg = pe.alloc_register("pe_last")
            before_reg = pe.alloc_register("pe_before")
            pe.reg_mov(done_reg, 2 * NC)
            pe.reg_mov(last_reg, 0)
            pe.reg_mov(before_reg, 0)
            with pe.Fori(1, NC) as turn_no:
                r = row_of(pe, turn_no)
                done = pe.snap(done_reg)
                acc_at = pe.snap(CH * (turn_no % 2))
                lowest = pe.snap(NC - blocks_of(r))
                slots = [pe.snap(GW * ((done // 2 + i) % ROW_SPL)) for i in range(ROW_SPL)]

                def block_of(q):
                    j = NC - 1 - q
                    at = slots[j % ROW_SPL]
                    for h in range(2):
                        pe.reg_mov(done_reg, pe.snap(done_reg) + 1)
                        pe.wait_ge(lo_ready, 2 * (NA - NC) + pe.snap(done_reg))
                        aggregate(acc[:, bass.ds(acc_at, CH)], h2_hi, h2_lo, q, h,
                                  lambda t: (hi_slots[:, bass.ds(at + t * CH, CH)],
                                             lo_slots[:, bass.ds(at + t * CH, CH)]), j == 0)\
                            .then_inc(adj_used, 1)

                block_of(NC - 1)
                with pe.If(turn_no >= 2):
                    gates(pe.snap(before_reg))
                pe.wait_ge(w_ready, 1)
                message(pe.snap(last_reg))
                turn_state(pe.snap(last_reg))
                for q in range(NC - 2, 1, -1):
                    with pe.If(lowest <= q):
                        block_of(q)
                pe.reg_mov(before_reg, pe.snap(last_reg))
                pe.reg_mov(last_reg, turn_no)
            gates(NC - 2)
            message(NC - 1)
            turn_state(NC - 1)
            gates(NC - 1)


def kernel(x, adj, L0_gnn_h, L1_gnn_W_msg, L1_gnn_b_msg, L1_gnn_W_ih, L1_gnn_W_hh, L1_gnn_b_ih, L1_gnn_b_hh):
    import numpy as np
    import concourse.bacc as bacc
    from concourse.bass_utils import run_bass_kernel_spmd

    a = np.asarray
    blocks = a(adj).reshape(NC, CH, NC, JT, P).transpose(0, 2, 4, 3, 1)[:, ::-1].reshape(NA, P, GW)
    arrays = {
        "adj_in": blocks,
        "x_rows_in": a(x).reshape(NC, JT, P, P).transpose(0, 2, 1, 3).reshape(NC, P, HW),
        "x_cols_in": a(x).reshape(NC, CH, P).transpose(0, 2, 1),
        "h_cols_in": a(L0_gnn_h).reshape(NC, CH, P).transpose(0, 2, 1),
        "weights_in": np.concatenate([a(L1_gnn_W_msg), a(L1_gnn_W_ih), a(L1_gnn_W_hh)], 0).reshape(7, P, P).transpose(2, 0, 1),
        "biases_in": np.concatenate([a(L1_gnn_b_msg), a(L1_gnn_b_ih), a(L1_gnn_b_hh)], 0).reshape(7, P).transpose(1, 0),
        "identity_in": np.eye(P, dtype=np.float32),
    }
    arrays = {name: np.ascontiguousarray(v) for name, v in arrays.items()}
    nc = bacc.Bacc("TRN2", target_bir_lowering=False, num_devices=1)
    args = [nc.dram_tensor(name, v.shape, FP32, kind="ExternalInput").ap() for name, v in arrays.items()]
    out = nc.dram_tensor("out_cols", (NC, P, CH), FP32, kind="ExternalOutput").ap()
    gnn_program(nc, *args, out)
    r = run_bass_kernel_spmd(nc, [arrays], core_ids=[0])
    return np.ascontiguousarray(a(r.results[0]["out_cols"]).transpose(0, 2, 1).reshape(N, P))
```

```python
from contextlib import ExitStack

import concourse.bass as bass
from concourse import mybir

FP32 = mybir.dt.float32
FP32R = mybir.dt.float32r
ALU = mybir.AluOpType
ACT = mybir.ActivationFunctionType

P = 128
N = 8192
CH = 512
JT = 4
NC = N // CH
GW = JT * CH
RAW = 4
SPL = 2
ROW_RAW = 6
ROW_SPL = 3
XS = 8
HT = JT // 2
HALF = HT * CH
HW = JT * P
NA = NC * NC
HELD = NC - 1 - GW // HW
NB = NC * (NC + 1) // 2 - HELD
EARLY = 3
DIAG_AT = 5
ALPHA = 0.1
EPS = 1e-5
MSG, I_R, I_Z, I_N, H_R, H_Z, H_N = range(7)


def gnn_program(nc, adj, x_rows, x_cols, h_cols, weights, biases, identity, out):
    x2_spill = nc.dram_tensor("x2_spill", (NC, P, CH), FP32).ap()
    part_spill = nc.dram_tensor("part_spill", (NC, P, CH), FP32).ap()
    ctx = ExitStack()
    with ctx:
        at = [-(-nc.sbuf_base // 64) * 64]

        def place(name, shape, dtype=FP32, offset=None):
            size = 4
            for n in shape[1:]:
                size *= n
            if offset is None:
                offset, at[0] = at[0], at[0] + -(-size // 64) * 64
            return nc.alloc_sbuf_tensor_at(name, shape, dtype, offset=offset)

        h1_at = at[0]
        h1_hi = place("h1_hi", [P, NC, HW], FP32R)
        h1_lo = place("h1_lo", [P, NC, HW], FP32R)
        raw = place("raw", [P, RAW, GW])
        power = place("power", [P, JT])
        epsilon = place("epsilon", [P, JT])
        carrier = place("carrier", [P, 1])
        act_carrier = place("act_carrier", [P, 1])
        bias = place("bias", [P, 7])
        gate_bias = place("gate_bias", [P, 2])
        ident = place("ident", [P, P])
        h2_hi = place("h2_hi", [P, NC, HW], FP32R)
        split_hi = place("split_hi", [P, (SPL + 1) * GW], FP32R, offset=at[0] - 4 * GW)
        pass_b_hi_at = at[0]
        at[0] += 4 * SPL * GW
        pass_b_hi_end = h2_lo_at = at[0]
        h2_lo = place("h2_lo", [P, NC, HW], FP32R)
        x_in = place("x_in", [P, NC, HW], offset=h2_lo_at)
        split_lo = place("split_lo", [P, (SPL + 1) * GW], FP32R, offset=at[0] - 4 * GW)
        pass_b_lo_at = at[0]
        at[0] += 4 * SPL * GW
        h1_now = place("h1_now", [P, 2, HW], offset=at[0] - 4 * 2 * HW)
        parts = place("parts", [P, 2, JT, 6])
        moments = place("moments", [P, 2, JT, 2])
        var_eps = place("var_eps", [P, 2, JT])
        rstd = place("rstd", [P, 2, JT])
        xc_in = place("xc_in", [P, CH])
        hc_in = place("hc_in", [P, CH])
        x_mix = place("x_mix", [P, CH])
        x2 = place("x2", [P, CH])
        normed = place("normed", [P, HW])
        part_out = place("part_out", [P, CH])
        assert at[0] <= nc.sbuf_usable_end
        raw_more = place("raw_more", [P, ROW_RAW - RAW, GW], offset=h1_at)
        row_hi = place("row_hi", [P, ROW_SPL, GW], FP32R, offset=h1_at + 4 * GW * (ROW_RAW - RAW))
        row_lo = place("row_lo", [P, ROW_SPL, GW], FP32R, offset=h1_at + 4 * GW * (ROW_RAW - RAW + ROW_SPL))
        assert ROW_RAW - RAW + 2 * ROW_SPL <= 2 * NC * HW // GW
        at[0] = pass_b_hi_at
        w_hi = place("w_hi", [P, 7, P], FP32R)
        w_lo = place("w_lo", [P, 7, P], FP32R)
        w_raw = place("w_raw", [P, 7, P], offset=at[0])
        state = place("state", [P, 2 * CH])
        reset = place("reset", [P, CH])
        update = place("update", [P, CH])
        assert at[0] <= pass_b_hi_end
        at[0] = pass_b_lo_at
        part_in = place("part_in", [P, 2 * CH])
        agg = place("agg", [P, CH])
        agg_hi = place("agg_hi", [P, CH], FP32R)
        agg_lo = place("agg_lo", [P, CH], FP32R)
        msg = place("msg", [P, CH])
        msg_hi = place("msg_hi", [P, CH], FP32R)
        msg_lo = place("msg_lo", [P, CH], FP32R)
        h2_sum = place("h2_sum", [P, HW])
        state_hi = place("state_hi", [P, CH], FP32R)
        state_lo = place("state_lo", [P, CH], FP32R)
        new = place("new", [P, CH])
        pre = place("pre", [P, CH])
        x2_in = place("x2_in", [P, CH])
        result = place("result", [P, CH])
        assert at[0] <= nc.sbuf_usable_end

        def bank(name, shape):
            return ctx.enter_context(nc.psum_tensor(name, shape, FP32))

        acc = bank("acc", [P, 2 * CH])
        acc2 = bank("acc2", [P, 2 * CH])
        msg_acc, g_hn = acc2[:, 0:CH], acc2[:, CH:2 * CH]
        turned = bank("turned", [P, CH])
        g_r = bank("g_r", [P, CH])
        g_z = bank("g_z", [P, CH])
        g_in = bank("g_in", [P, CH])

        def sem(name):
            return ctx.enter_context(nc.semaphore(name))

        x_landed = [sem(f"x_landed{i}") for i in range(XS)]
        raw_landed = [sem(f"raw_landed{i}") for i in range(ROW_RAW)]
        const_landed = sem("const_landed")
        cols_landed = sem("cols_landed")
        power_set = sem("power_set")
        hi_ready = sem("hi_ready")
        lo_ready = sem("lo_ready")
        adj_used = sem("adj_used")
        parts_ready = sem("parts_ready")
        moments_ready = sem("moments_ready")
        eps_added = sem("eps_added")
        rstd_ready = sem("rstd_ready")
        h1_now_ready = sem("h1_now_ready")
        normed_ready = sem("normed_ready")
        h_hi_ready = sem("h_hi_ready")
        h_ready = sem("h_ready")
        mix_ready = sem("mix_ready")
        x2_ready = sem("x2_ready")
        x2_stored = sem("x2_stored")
        x2_turned = sem("x2_turned")
        diag_used = sem("diag_used")
        part_ready = sem("part_ready")
        part_stored = sem("part_stored")
        w_landed = sem("w_landed")
        w_hi_ready = sem("w_hi_ready")
        w_ready = sem("w_ready")
        bias_ready = sem("bias_ready")
        part_landed = sem("part_landed")
        sum_ready = sem("sum_ready")
        state_turned = sem("state_turned")
        state_out = sem("state_out")
        state_hi_ready = sem("state_hi_ready")
        state_ready = sem("state_ready")
        agg_out = sem("agg_out")
        agg_hi_ready = sem("agg_hi_ready")
        agg_ready = sem("agg_ready")
        msg_done = sem("msg_done")
        msg_out = sem("msg_out")
        msg_hi_ready = sem("msg_hi_ready")
        msg_ready = sem("msg_ready")
        reset_done = sem("reset_done")
        gates_done = sem("gates_done")
        reset_ready = sem("reset_ready")
        update_ready = sem("update_ready")
        pre_a_ready = sem("pre_a_ready")
        pre_ready = sem("pre_ready")
        new_ready = sem("new_ready")
        diff_ready = sem("diff_ready")
        mixed_ready = sem("mixed_ready")
        gru_ready = sem("gru_ready")
        x2_landed = sem("x2_landed")
        result_ready = sem("result_ready")
        out_stored = sem("out_stored")
        last_stored = sem("last_stored")

        def row(t, k):
            return t[k] if isinstance(k, int) else t[bass.ds(k, 1)].rearrange("o p n -> (o p) n")

        def group(table, k):
            return table[:, k, :] if isinstance(k, int) else table[:, bass.ds(k, 1), :].rearrange("p o n -> p (o n)")

        def row_slot(slot):
            return raw[:, slot, :] if slot < RAW else raw_more[:, slot - RAW, :]

        def row_split(m, slot, half):
            if isinstance(m, int) and m < SPL:
                at = GW * (1 + m % SPL) + HALF * half
                return split_hi[:, at:at + HALF], split_lo[:, at:at + HALF]
            part = slice(half * HALF, (half + 1) * HALF)
            return row_hi[:, slot % ROW_SPL, part], row_lo[:, slot % ROW_SPL, part]

        def half_of(table, turn):
            at = CH * (turn % 2)
            return table[:, at:at + CH] if isinstance(turn, int) else table[:, bass.ds(at, CH)]

        def row_of(eng, turn):
            r = (turn // 2 + (turn % 2) * (NC - 1 - 2 * (turn // 2))) % NC
            return r if isinstance(turn, int) else eng.snap(r)

        def blocks_of(r):
            return NC - 1 - r + (r > HELD)

        def group_at(c, p):
            return (c + 1 + p) % NC if isinstance(c, int) and 1 <= c <= EARLY else p

        def split_slot(eng, c, p):
            at = GW * (1 + p % SPL)
            if isinstance(c, int):
                return 0 if group_at(c, p) == c <= HELD else at
            return at if p == 0 or p > HELD else eng.snap((c != p) * at)

        def rows_of_pass_b(eng, name, split, first, second, third):
            last = eng.alloc_register(name + "_last")
            before = eng.alloc_register(name + "_before")
            first_at = eng.alloc_register(name + "_first_at")
            second_at = eng.alloc_register(name + "_second_at")
            third_at = eng.alloc_register(name + "_third_at")
            for register, value in ((last, 0), (before, 0), (first_at, NC), (second_at, NB), (third_at, NB)):
                eng.reg_mov(register, value)
            first_blocks = NB % ROW_RAW
            with eng.Fori(0, NB // ROW_RAW) as rounds:
                for u in range(ROW_RAW):
                    m = ROW_RAW * rounds + first_blocks + u
                    split(m, (first_blocks + u) % ROW_RAW)
                    with eng.If(m == eng.snap(second_at)):
                        second(last, before)
                    with eng.If(m == eng.snap(third_at)):
                        third(last, before)
                        eng.reg_mov(before, eng.snap(last))
                        eng.reg_mov(last, eng.snap(last) + 1)
                    with eng.If(m == eng.snap(first_at)):
                        first(last, before, m)
                        blocks = eng.snap(blocks_of(row_of(eng, eng.snap(last) + 1)))
                        eng.reg_mov(second_at, m + 2 - (blocks < 2))
                        eng.reg_mov(third_at, m + 3 - (blocks < 2) - (blocks < 3))
                        eng.reg_mov(first_at, m + blocks)

        block = ctx.enter_context(nc.Block())

        @block.sync
        def _(sp):
            def load_x(q):
                sp.dma_start(x_in[:, q, :], x_rows[q]).then_inc(x_landed[q % XS], 16)

            def load_block(c, p):
                before = NC * c + p - RAW
                if isinstance(c, int):
                    if 0 <= before < NC:
                        sp.wait_ge(adj_used, 2 * (before + 1))
                    if before >= NC:
                        sp.wait_ge(lo_ready, 2 * (before - NC + 1))
                else:
                    sp.wait_ge(lo_ready, 2 * (before - NC + 1))
                block = NC * c + NC - 1 - group_at(c, p)
                source = adj[block] if isinstance(c, int) else row(adj, sp.snap(block))
                sp.dma_start(raw[:, p % RAW, :], source).then_inc(raw_landed[p % RAW], 16)

            def load_cols(c):
                if not isinstance(c, int):
                    sp.wait_ge(mix_ready, c)
                sp.dma_start(xc_in[:, :], row(x_cols, c)).then_inc(cols_landed, 16)
                sp.dma_start(hc_in[:, :], row(h_cols, c)).then_inc(cols_landed, 16)

            def store_x2(k):
                sp.wait_ge(x2_ready, k + 1)
                sp.dma_start(row(x2_spill, k), x2[:, :]).then_inc(x2_stored, 16)

            def store_part(k):
                sp.wait_ge(part_ready, k + 2)
                sp.dma_start(row(part_spill, k), part_out[:, :]).then_inc(part_stored, 16)

            for q in range(4):
                load_x(q)
            for q in range(NC):
                load_block(0, q)
                if q + 4 < NC:
                    load_x(q + 4)
            load_cols(0)
            sp.dma_start(ident[:, :], identity).then_inc(const_landed, 16)
            sp.dma_start(bias[:, :], biases).then_inc(const_landed, 16)

            def chunk(c):
                for p in range(NC):
                    load_block(c, p)
                    if p == 6:
                        store_x2(c - 1)
                        if not isinstance(c, int) or c >= 2:
                            store_part(c - 2)
                    if p == 8:
                        load_cols(c)

            for c in range(1, EARLY + 1):
                chunk(c)
            with sp.Fori(EARLY + 1, NC) as c:
                chunk(c)

            first_blocks = [(m + 1) % NC for m in range(NC)]
            for turn in range(1, NC):
                r = row_of(sp, turn)
                first_blocks += [NC * r + i for i in range(blocks_of(r))]
            peeled = NC + (NB - NC) % ROW_RAW

            def load_first(m):
                if m < RAW:
                    sp.wait_ge(lo_ready, 2 * (NA - NC + m - RAW + 1))
                elif m >= ROW_RAW:
                    sp.wait_ge(lo_ready, 2 * (NA - NC + m - ROW_RAW + 1))
                slot = m % ROW_RAW
                sp.dma_start(row_slot(slot), adj[first_blocks[m]]).then_inc(raw_landed[slot], 16)

            groups = (ROW_RAW - RAW) * GW // HW
            assert groups <= NC
            sp.wait_ge(adj_used, 2 * (NA - NC + groups))
            for m in range(RAW, ROW_RAW):
                load_first(m)
            for m in range(RAW):
                load_first(m)
                if m == 2:
                    store_part(NC - 2)
            for m in range(ROW_RAW, peeled):
                load_first(m)
                if m == ROW_RAW + 1:
                    store_x2(NC - 1)
                    store_part(NC - 1)
                    sp.wait_ge(adj_used, 2 * (NA + SPL))
                    sp.dma_start(w_raw[:, :, :], weights).then_inc(w_landed, 16)

            block_reg = sp.alloc_register("block_reg")
            left_reg = sp.alloc_register("left_reg")
            turn_reg = sp.alloc_register("turn_reg")
            assert NC + 1 <= peeled < NC + 1 + blocks_of(1)
            sp.reg_mov(block_reg, first_blocks[peeled])
            sp.reg_mov(left_reg, NC + 1 + blocks_of(1) - peeled)
            sp.reg_mov(turn_reg, 2)

            with sp.Fori(0, (NB - peeled) // ROW_RAW) as rounds:
                for u in range(ROW_RAW):
                    m = ROW_RAW * rounds + peeled + u
                    slot = (peeled + u) % ROW_RAW
                    sp.wait_ge(lo_ready, 2 * (NA - NC + m - ROW_RAW + 1))
                    sp.dma_start(row_slot(slot), row(adj, sp.snap(block_reg))).then_inc(raw_landed[slot], 16)
                    sp.reg_mov(block_reg, sp.snap(block_reg) + 1)
                    sp.reg_mov(left_reg, sp.snap(left_reg) - 1)
                    with sp.If(sp.snap(left_reg) == 0):
                        turn = sp.snap(turn_reg) + 1
                        sp.reg_mov(turn_reg, turn)
                        r = row_of(sp, turn)
                        sp.reg_mov(block_reg, NC * r)
                        sp.reg_mov(left_reg, blocks_of(r))
            sp.wait_ge(result_ready, NC)
            sp.dma_start(out[row_of(sp, NC - 1)], pre[:, :]).then_inc(last_stored, 16)
            sp.wait_ge(last_stored, 16)

        @block.gpsimd
        def _(pool):
            pool.memset(power[:, :], -0.5).then_inc(power_set, 1)
            pool.memset(epsilon[:, :], EPS).then_inc(power_set, 1)
            pool.memset(part_out[:, :], 0.0).then_inc(part_ready, 2)

            def inverse_deviation(n, b):
                pool.wait_ge(moments_ready, n + 1)
                pool.tensor_tensor(var_eps[:, b, :], moments[:, b, :, 1], epsilon[:, :], ALU.add).then_inc(eps_added, 1)
                pool.wait_ge(eps_added, n + 1)
                pool.tensor_tensor(rstd[:, b, :], var_eps[:, b, :], power[:, :], ALU.pow).then_inc(rstd_ready, 1)

            pool.wait_ge(power_set, 2)
            for q in range(NC):
                inverse_deviation(q, q % 2)
            with pool.Fori(1, NC) as c:
                inverse_deviation(NC + c - 1, 0)
            inverse_deviation(2 * NC - 1, 0)

            pool.wait_ge(h_ready, 2 * NC)
            pool.wait_ge(adj_used, 2 * (NA + SPL))
            pool.wait_ge(x2_stored, 16 * NC)
            pool.wait_ge(part_stored, 16 * NC)
            pool.memset(update[:, 0:1], 0.0).then_inc(diff_ready, 2)
            pool.memset(new[:, 0:1], 0.0).then_inc(gru_ready, 1)

            def sum_state(k):
                if not isinstance(k, int) or k:
                    pool.wait_ge(state_turned, k)
                r = row_of(pool, k)
                pool.tensor_tensor(h2_sum[:, :], group(h2_hi, r).bitcast(FP32), group(h2_lo, r).bitcast(FP32),
                                   ALU.add).then_inc(sum_ready, 1)

            def load_part(k):
                if not isinstance(k, int) or k >= 2:
                    pool.wait_ge(agg_out, k - 1)
                if not isinstance(k, int) or k:
                    pool.wait_ge(part_landed, 16 * k)
                pool.dma_start(half_of(part_in, k), row(part_spill, row_of(pool, k))).then_inc(part_landed, 16)

            def load_x2(k):
                if not isinstance(k, int) or k:
                    pool.wait_ge(result_ready, k)
                pool.dma_start(x2_in[:, :], row(x2_spill, row_of(pool, k))).then_inc(x2_landed, 16)

            def new_state(k):
                if not isinstance(k, int) or k:
                    pool.wait_ge(out_stored, 16 * k)
                pool.wait_ge(new_ready, k + 1)
                pool.tensor_tensor(result[:, :], half_of(state, k), new[:, :], ALU.subtract).then_inc(diff_ready, 1)
                pool.wait_ge(update_ready, k + 1)
                pool.wait_ge(diff_ready, k + 3)
                pool.tensor_tensor(result[:, :], result[:, :], update[:, :], ALU.mult).then_inc(mixed_ready, 1)
                pool.wait_ge(mixed_ready, k + 1)
                pool.tensor_tensor(result[:, :], result[:, :], new[:, :], ALU.add).then_inc(gru_ready, 1)
                pool.wait_ge(x2_landed, 16 * (k + 1))
                pool.wait_ge(gru_ready, k + 2)
                pool.tensor_tensor(result[:, :], result[:, :], x2_in[:, :], ALU.add).then_inc(result_ready, 1)

            def store_result(k):
                pool.wait_ge(result_ready, k + 1)
                pool.dma_start(row(out, row_of(pool, k)), result[:, :]).then_inc(out_stored, 16)

            load_part(0)
            sum_state(0)
            load_x2(0)
            load_part(1)
            pool.wait_ge(w_landed, 16)
            pool.tensor_copy(w_hi[:, :, :], w_raw[:, :, :]).then_inc(w_hi_ready, 1)
            pool.wait_ge(w_hi_ready, 1)
            pool.tensor_tensor(w_lo[:, :, :], w_raw[:, :, :], w_hi[:, :, :].bitcast(FP32), ALU.subtract)\
                .then_inc(w_ready, 1)
            load_part(2)
            sum_state(1)

            def turn(k):
                if not isinstance(k, int) or k < NC - 1:
                    load_part(k + 1)
                sum_state(k)
                new_state(k - 2)
                store_result(k - 2)
                load_x2(k - 1)

            turn(2)
            with pool.Fori(3, NC - 1) as k:
                turn(k)
            turn(NC - 1)
            new_state(NC - 2)
            store_result(NC - 2)
            load_x2(NC - 1)
            pool.wait_ge(x2_landed, 16 * NC)
            pool.wait_ge(new_ready, NC)
            pool.tensor_tensor(x2_in[:, :], new[:, :], x2_in[:, :], ALU.add).then_inc(gru_ready, 1)
            pool.wait_ge(out_stored, 16 * (NC - 1))

        @block.scalar
        def _(act):
            act.preload_act_table(ACT.Sigmoid)

            def hi_part(c, p):
                g, slot = NC * c + p, p % RAW
                if isinstance(c, int):
                    if group_at(c, p) == c >= 2:
                        act.wait_ge(diag_used, c - 1)
                elif EARLY < p <= HELD:
                    with act.If(c == p):
                        act.wait_ge(diag_used, p - 1)
                        act.activation(act_carrier[:, :], rstd[:, 0, 0:1], ACT.Copy)
                act.wait_ge(raw_landed[slot], 16 * ((NC // RAW) * c + p // RAW + 1))
                at = split_slot(act, c, p)
                for h in range(2):
                    if not isinstance(g, int) or g >= NC + SPL:
                        act.wait_ge(adj_used, 2 * (g - SPL) + h + 1)
                    act.activation(split_hi[:, bass.ds(at + h * HALF, HALF)],
                                   raw[:, slot, h * HALF:(h + 1) * HALF], ACT.Copy).then_inc(hi_ready, 1)

            def row_hi_part(m, slot):
                loads = (m - slot) // ROW_RAW + 1 + (NA // RAW if slot < RAW else 0)
                act.wait_ge(raw_landed[slot], 16 * loads)
                for h in range(2):
                    if isinstance(m, int) and SPL <= m < SPL + ROW_SPL:
                        act.wait_ge(adj_used, 2 * NA)
                    else:
                        before = SPL if isinstance(m, int) and m < SPL else ROW_SPL
                        act.wait_ge(adj_used, 2 * (NA + m - before) + h + 1)
                    act.activation(row_split(m, slot, h)[0], row_slot(slot)[:, h * HALF:(h + 1) * HALF], ACT.Copy)\
                        .then_inc(hi_ready, 1)

            def h1_hi_part(q):
                act.wait_ge(normed_ready, q + 1)
                if q >= 2:
                    act.wait_ge(adj_used, 2 * (q - 1))
                    act.wait_ge(h_ready, q - 1)
                act.activation(h1_now[:, q % 2, :], normed[:, :], ACT.Relu).then_inc(h1_now_ready, 1)
                act.wait_ge(h1_now_ready, q + 1)
                act.activation(h1_hi[:, q, :], h1_now[:, q % 2, :], ACT.Copy).then_inc(h_hi_ready, 1)

            def h_hi(n, table, k):
                act.wait_ge(normed_ready, n + 1)
                to = table[:, k, :] if isinstance(k, int) else \
                    table[:, bass.ds(k, 1), :].rearrange("p o n -> p (o n)")
                act.activation(to, normed[:, :], ACT.Relu).then_inc(h_hi_ready, 1)

            def part_evac(k):
                if isinstance(k, int) and k == NC - 1:
                    act.wait_ge(adj_used, 2 * NA)
                act.wait_ge(part_stored, 16 * k)
                src = acc2[:, CH * (k % 2):CH * (k % 2) + CH] if isinstance(k, int) else \
                    acc2[:, bass.ds(CH * (k % 2), CH)]
                act.activation(part_out[:, :], src, ACT.Copy).then_inc(part_ready, 1)

            for q in range(NC):
                h1_hi_part(q)

            def chunk(c):
                for p in range(NC):
                    hi_part(c, p)
                    if p == 3:
                        h_hi(NC + c - 1, h2_hi, c - 1)
                    if p == NC - 1 and not (isinstance(c, int) and c == 1):
                        part_evac(c - 1)

            for c in range(1, EARLY + 1):
                chunk(c)
            with act.Fori(EARLY + 1, NC) as c:
                chunk(c)

            for m in range(NB % ROW_RAW):
                row_hi_part(m, m)
                if m == 1:
                    part_evac(NC - 1)
            h_hi(2 * NC - 1, h2_hi, NC - 1)

            def msg_part(k):
                act.wait_ge(msg_done, k + 1)
                act.activation(msg[:, :], msg_acc, ACT.Relu, bias=bias[:, MSG:MSG + 1]).then_inc(msg_out, 1)
                act.wait_ge(msg_out, k + 1)
                act.activation(msg_hi[:, :], msg[:, :], ACT.Copy).then_inc(msg_hi_ready, 1)

            def sigmoids(k):
                act.wait_ge(reset_done, k + 1)
                act.activation(reset[:, :], g_r[:, :], ACT.Sigmoid, bias=gate_bias[:, 0:1]).then_inc(reset_ready, 1)
                act.wait_ge(gates_done, k + 1)
                act.wait_ge(gru_ready, k + 1)
                act.activation(update[:, :], g_z[:, :], ACT.Sigmoid, bias=gate_bias[:, 1:2]).then_inc(update_ready, 1)

            def new_state(k):
                act.wait_ge(pre_ready, k + 1)
                act.activation(new[:, :], pre[:, :], ACT.Tanh, bias=bias[:, I_N:I_N + 1]).then_inc(new_ready, 1)

            def state_part(k):
                act.wait_ge(state_turned, k + 1)
                act.wait_ge(diff_ready, k + 1)
                act.activation(half_of(state, k), turned[:, :], ACT.Copy).then_inc(state_out, 1)
                act.activation(state_hi[:, :], turned[:, :], ACT.Copy).then_inc(state_hi_ready, 1)

            def first(last, before, m):
                with act.If(act.snap(last) >= 1):
                    msg_part(act.snap(before))

            def second(last, before):
                with act.If(act.snap(last) >= 1):
                    sigmoids(act.snap(before))

            def third(last, before):
                with act.If(act.snap(last) >= 1):
                    new_state(act.snap(before))
                state_part(act.snap(last))

            rows_of_pass_b(act, "act", row_hi_part, first, second, third)
            msg_part(NC - 2)
            sigmoids(NC - 2)
            new_state(NC - 2)
            state_part(NC - 1)
            msg_part(NC - 1)
            sigmoids(NC - 1)
            new_state(NC - 1)

        @block.vector
        def _(dve):
            def lo_part(c, p):
                g, slot = NC * c + p, p % RAW
                at = split_slot(dve, c, p)
                for h in range(2):
                    if isinstance(c, int) and (c, p, h) == (1, SPL - 1, 1):
                        dve.wait_ge(adj_used, 2 * NC)
                        dve.wait_ge(h_ready, NC)
                    dve.wait_ge(hi_ready, 2 * (g - NC) + h + 1)
                    half = bass.ds(at + h * HALF, HALF)
                    dve.tensor_tensor(split_lo[:, half], raw[:, slot, h * HALF:(h + 1) * HALF],
                                      split_hi[:, half].bitcast(FP32), ALU.subtract).then_inc(lo_ready, 1)

            def row_lo_part(m, slot):
                for h in range(2):
                    dve.wait_ge(hi_ready, 2 * (NA - NC + m) + h + 1)
                    hi, lo = row_split(m, slot, h)
                    dve.tensor_tensor(lo, row_slot(slot)[:, h * HALF:(h + 1) * HALF], hi.bitcast(FP32),
                                      ALU.subtract).then_inc(lo_ready, 1)

            def statistics(n, rows, b):
                for t in range(JT):
                    last = dve.bn_stats(parts[:, b, t, :], rows[:, t * P:(t + 1) * P])
                last.then_inc(parts_ready, 1)
                dve.wait_ge(parts_ready, n + 1)
                dve.memset(carrier[:, :], 0.0)
                for t in range(JT):
                    last = dve.bn_aggr(moments[:, b, t, :], parts[:, b, t, :])
                last.then_inc(moments_ready, 1)

            def normalise(n, rows, b):
                if isinstance(n, int) and 0 < n < NC:
                    dve.wait_ge(h1_now_ready, n)
                elif not isinstance(n, int) or n:
                    dve.wait_ge(h_ready, n)
                dve.wait_ge(rstd_ready, n + 1)
                for t in range(JT):
                    last = dve.tensor_scalar(normed[:, t * P:(t + 1) * P], rows[:, t * P:(t + 1) * P],
                                             moments[:, b, t, 0:1], rstd[:, b, t:t + 1], ALU.subtract, ALU.mult)
                last.then_inc(normed_ready, 1)

            def h_lo(n, hi_table, lo_table, k):
                dve.wait_ge(h_hi_ready, n + 1)
                if isinstance(k, int):
                    hi, lo = hi_table[:, k, :], lo_table[:, k, :]
                else:
                    hi = hi_table[:, bass.ds(k, 1), :].rearrange("p o n -> p (o n)")
                    lo = lo_table[:, bass.ds(k, 1), :].rearrange("p o n -> p (o n)")
                dve.scalar_tensor_tensor(lo, normed[:, :], 0.0, hi.bitcast(FP32), ALU.max, ALU.subtract)\
                    .then_inc(h_ready, 1)

            def statistics_x(q):
                dve.wait_ge(x_landed[q % XS], 16 * (q // XS + 1))
                statistics(q, x_in[:, q, :], q % 2)

            def h1_lo_part(q):
                dve.wait_ge(h_hi_ready, q + 1)
                dve.tensor_tensor(h1_lo[:, q, :], h1_now[:, q % 2, :], h1_hi[:, q, :].bitcast(FP32), ALU.subtract)\
                    .then_inc(h_ready, 1)

            statistics_x(0)
            statistics_x(1)
            normalise(0, x_in[:, 0, :], 0)
            for q in range(NC):
                if q + 1 < NC:
                    normalise(q + 1, x_in[:, q + 1, :], (q + 1) % 2)
                if q + 2 < NC:
                    statistics_x(q + 2)
                h1_lo_part(q)

            def mix(c):
                dve.wait_ge(cols_landed, 32 * (c + 1))
                if not isinstance(c, int) or c:
                    dve.wait_ge(x2_ready, c)
                dve.scalar_tensor_tensor(x_mix[:, :], hc_in[:, :], ALPHA, xc_in[:, :], ALU.mult, ALU.add)\
                    .then_inc(mix_ready, 1)

            mix(0)

            def x2_evac(k):
                dve.wait_ge(adj_used, 2 * NC * (k + 1))
                dve.wait_ge(mix_ready, k + 1)
                if not isinstance(k, int) or k:
                    dve.wait_ge(x2_stored, 16 * k)
                src = acc[:, CH * (k % 2):CH * (k % 2) + CH] if isinstance(k, int) else \
                    acc[:, bass.ds(CH * (k % 2), CH)]
                dve.scalar_tensor_tensor(x2[:, :], src, 1.0 - ALPHA, x_mix[:, :], ALU.mult, ALU.add)\
                    .then_inc(x2_ready, 1)

            def x2_statistics(k):
                dve.wait_ge(x2_turned, k + 1)
                statistics(NC + k, turned[:, :], 0)

            def chunk(c):
                for p in range(NC):
                    lo_part(c, p)
                    if p == 0:
                        x2_evac(c - 1)
                    if p == 1:
                        x2_statistics(c - 1)
                    if p == 2:
                        normalise(NC + c - 1, turned[:, :], 0)
                    if p == 3:
                        h_lo(NC + c - 1, h2_hi, h2_lo, c - 1)
                    if p == NC - 4:
                        mix(c)

            for c in range(1, EARLY + 1):
                chunk(c)
            with dve.Fori(EARLY + 1, NC) as c:
                chunk(c)

            for m in range(NB % ROW_RAW):
                row_lo_part(m, m)
                if m == 0:
                    x2_evac(NC - 1)
                if m == 1:
                    x2_statistics(NC - 1)
                if m == 2:
                    normalise(2 * NC - 1, turned[:, :], 0)
            h_lo(2 * NC - 1, h2_hi, h2_lo, NC - 1)
            dve.wait_ge(const_landed, 32)
            dve.tensor_tensor(gate_bias[:, :], bias[:, I_R:I_Z + 1], bias[:, H_R:H_Z + 1], ALU.add)\
                .then_inc(bias_ready, 1)

            def agg_evac(k, blocks_done):
                dve.wait_ge(adj_used, 2 * blocks_done)
                dve.wait_ge(part_landed, 16 * (k + 1))
                dve.tensor_tensor(agg[:, :], half_of(acc, k), half_of(part_in, k), ALU.add).then_inc(agg_out, 1)
                dve.wait_ge(agg_out, k + 1)
                dve.tensor_copy(agg_hi[:, :], agg[:, :]).then_inc(agg_hi_ready, 1)
                dve.wait_ge(agg_hi_ready, k + 1)
                dve.tensor_tensor(agg_lo[:, :], agg[:, :], agg_hi[:, :].bitcast(FP32), ALU.subtract)\
                    .then_inc(agg_ready, 1)

            def msg_split(k):
                dve.wait_ge(msg_hi_ready, k + 1)
                dve.tensor_tensor(msg_lo[:, :], msg[:, :], msg_hi[:, :].bitcast(FP32), ALU.subtract)\
                    .then_inc(msg_ready, 1)

            def new_input(k):
                dve.wait_ge(reset_ready, k + 1)
                dve.scalar_tensor_tensor(pre[:, :], g_hn, bias[:, H_N:H_N + 1], reset[:, :],
                                         ALU.add, ALU.mult).then_inc(pre_a_ready, 1)
                dve.wait_ge(gates_done, k + 1)
                dve.wait_ge(pre_a_ready, k + 1)
                dve.tensor_tensor(pre[:, :], pre[:, :], g_in[:, :], ALU.add).then_inc(pre_ready, 1)

            def state_split(k):
                dve.wait_ge(state_hi_ready, k + 1)
                dve.tensor_tensor(state_lo[:, :], half_of(state, k), state_hi[:, :].bitcast(FP32), ALU.subtract)\
                    .then_inc(state_ready, 1)

            def first(last, before, m):
                with dve.If(dve.snap(last) >= 1):
                    msg_split(dve.snap(before))
                agg_evac(dve.snap(last), NA + m)

            def second(last, before):
                with dve.If(dve.snap(last) >= 1):
                    new_input(dve.snap(before))

            def third(last, before):
                state_split(dve.snap(last))

            rows_of_pass_b(dve, "dve", row_lo_part, first, second, third)
            msg_split(NC - 2)
            new_input(NC - 2)
            state_split(NC - 1)
            agg_evac(NC - 1, NA + NB)
            msg_split(NC - 1)
            new_input(NC - 1)
            dve.wait_ge(new_ready, NC)
            dve.tensor_tensor(pre[:, :], half_of(state, NC - 1), new[:, :], ALU.subtract).then_inc(diff_ready, 1)
            dve.wait_ge(update_ready, NC)
            dve.wait_ge(diff_ready, NC + 2)
            dve.tensor_tensor(pre[:, :], pre[:, :], update[:, :], ALU.mult).then_inc(mixed_ready, 1)
            dve.wait_ge(mixed_ready, NC)
            dve.wait_ge(gru_ready, NC + 1)
            dve.tensor_tensor(pre[:, :], pre[:, :], x2_in[:, :], ALU.add).then_inc(result_ready, 1)

        @block.tensor
        def _(pe):
            def product(to, w_hi, w_lo, m_hi, m_lo, start):
                pe.matmul(to, w_hi, m_hi, start=start, stop=False, skip_group_check=True)
                pe.matmul(to, w_lo, m_hi, start=False, stop=False, skip_group_check=True)
                return pe.matmul(to, w_hi, m_lo, start=False, stop=False, skip_group_check=True)

            def aggregate(to, hi_table, lo_table, q, h, moving, start):
                for t in range(h * HT, (h + 1) * HT):
                    tile = slice(t * P, (t + 1) * P)
                    last = product(to, hi_table[:, q, tile], lo_table[:, q, tile], *moving(t), start and t == 0)
                return last

            def split_at(at):
                return lambda t: (split_hi[:, bass.ds(at + t * CH, CH)], split_lo[:, bass.ds(at + t * CH, CH)])

            def turn(src, ready, count, done):
                pe.wait_ge(ready, count)
                for t in range(JT):
                    last = pe.transpose(turned[:, t * P:(t + 1) * P], src[:, t * P:(t + 1) * P], ident[:, :])
                last.then_inc(done, 1)

            for q in range(NC):
                pe.wait_ge(h1_now_ready, q + 1)
                pe.wait_ge(raw_landed[q % RAW], 16 * (q // RAW + 1))
                for t in range(JT):
                    last = pe.matmul(acc[:, 0:CH], h1_now[:, q % 2, t * P:(t + 1) * P],
                                     raw[:, q % RAW, t * CH:(t + 1) * CH],
                                     start=q == 0 and t == 0, stop=False, skip_group_check=True)
                    if t % HT == HT - 1:
                        last.then_inc(adj_used, 1)
            pe.wait_ge(h_ready, NC)

            pe.wait_ge(const_landed, 32)
            def layer1(c, p, h):
                to = acc[:, bass.ds(bank_of(c), CH)]
                return aggregate(to, h1_hi, h1_lo, group_at(c, p), h, split_at(split_slot(pe, c, p)), p == 0)

            def layer2(c, p, h):
                q = group_at(c, p)
                to = acc2[:, bass.ds(bank_of(c), CH)]
                return aggregate(to, h2_hi, h2_lo, q, h, split_at(GW * (1 + p % SPL)), q == 0)

            def diagonal(q):
                to = acc2[:, CH * (q % 2):CH * (q % 2) + CH]
                aggregate(to, h2_hi, h2_lo, q, 0, split_at(0), False)
                aggregate(to, h2_hi, h2_lo, q, 1, split_at(0), False).then_inc(diag_used, 1)

            def bank_of(c):
                return CH * (c % 2) if isinstance(c, int) else pe.snap(CH * (c % 2))

            for c in range(1, EARLY + 1):
                for p in range(NC):
                    q = group_at(c, p)
                    if p == DIAG_AT and c >= 2:
                        pe.wait_ge(h_ready, NC + c)
                        diagonal(c - 1)
                    if q == 0:
                        pe.wait_ge(part_ready, c)
                    for h in range(2):
                        pe.wait_ge(lo_ready, 2 * (NC * (c - 1) + p) + h + 1)
                        if q < c:
                            pe.wait_ge(h_ready, NC + q + 1)
                            layer2(c, p, h)
                        layer1(c, p, h).then_inc(adj_used, 1)
                    if p == 0:
                        turn(x2, x2_ready, c, x2_turned)

            with pe.Fori(EARLY + 1, NC) as c:
                for h in range(2):
                    pe.wait_ge(lo_ready, 2 * NC * (c - 1) + h + 1)
                    layer1(c, 0, h)
                turn(x2, x2_ready, c, x2_turned)
                pe.wait_ge(part_ready, c)
                for h in range(2):
                    layer2(c, 0, h).then_inc(adj_used, 1)
                for q in range(1, NC):
                    with pe.If(c > q):
                        pe.wait_ge(h_ready, NC + q + 1)
                        if EARLY <= q <= HELD:
                            with pe.If(c == q + 1):
                                diagonal(q)
                        for h in range(2):
                            pe.wait_ge(lo_ready, 2 * (NC * (c - 1) + q) + h + 1)
                            layer2(c, q, h)
                    for h in range(2):
                        pe.wait_ge(lo_ready, 2 * (NC * (c - 1) + q) + h + 1)
                        layer1(c, q, h).then_inc(adj_used, 1)

            def gates_of_state(k):
                pe.wait_ge(state_ready, k + 1)
                for to, w in ((g_r, H_R), (g_z, H_Z), (g_hn, H_N)):
                    product(to[:, :], w_hi[:, w, :], w_lo[:, w, :], state_hi[:, :], state_lo[:, :], True)

            def gates_of_message(k):
                pe.wait_ge(msg_ready, k + 1)
                product(g_r[:, :], w_hi[:, I_R, :], w_lo[:, I_R, :], msg_hi[:, :], msg_lo[:, :], False)\
                    .then_inc(reset_done, 1)
                product(g_in[:, :], w_hi[:, I_N, :], w_lo[:, I_N, :], msg_hi[:, :], msg_lo[:, :], True)
                product(g_z[:, :], w_hi[:, I_Z, :], w_lo[:, I_Z, :], msg_hi[:, :], msg_lo[:, :], False)\
                    .then_inc(gates_done, 1)

            def gates(k):
                gates_of_state(k)
                gates_of_message(k)

            def message(k):
                pe.wait_ge(agg_ready, k + 1)
                product(msg_acc, w_hi[:, MSG, :], w_lo[:, MSG, :], agg_hi[:, :], agg_lo[:, :], True)\
                    .then_inc(msg_done, 1)

            def turn_state(k):
                turn(h2_sum, sum_ready, k + 1, state_turned)

            hi_slots, lo_slots = (a[:, :, :].rearrange("p s n -> p (s n)") for a in (row_hi, row_lo))

            def split_block(m, q, bank, start):
                for h in range(2):
                    pe.wait_ge(lo_ready, 2 * (NA - NC + m) + h + 1)
                    hi, lo = row_split(m, m % ROW_RAW, h)
                    aggregate(acc[:, CH * bank:CH * bank + CH], h2_hi, h2_lo, q, h,
                              lambda t: (hi[:, t % HT * CH:(t % HT + 1) * CH], lo[:, t % HT * CH:(t % HT + 1) * CH]),
                              start).then_inc(adj_used, 1)

            for m in range(NC - 1):
                split_block(m, NC - 2 - m, 0, m == 0)
                if m == 0:
                    turn(x2, x2_ready, NC, x2_turned)
            pe.wait_ge(h_ready, 2 * NC)
            split_block(NC - 1, NC - 1, 0, False)
            pe.wait_ge(part_ready, NC + 1)

            done_reg = pe.alloc_register("pe_done")
            last_reg = pe.alloc_register("pe_last")
            before_reg = pe.alloc_register("pe_before")
            pe.reg_mov(done_reg, 2 * NC)
            pe.reg_mov(last_reg, 0)
            pe.reg_mov(before_reg, 0)
            with pe.Fori(1, NC - 1) as turn_no:
                r = row_of(pe, turn_no)
                done = pe.snap(done_reg)
                acc_at = pe.snap(CH * (turn_no % 2))
                lowest = pe.snap(NC - blocks_of(r))
                slots = [pe.snap(GW * ((done // 2 + i) % ROW_SPL)) for i in range(ROW_SPL)]

                def block_of(q):
                    j = NC - 1 - q
                    at = slots[j % ROW_SPL]
                    for h in range(2):
                        pe.reg_mov(done_reg, pe.snap(done_reg) + 1)
                        pe.wait_ge(lo_ready, 2 * (NA - NC) + pe.snap(done_reg))
                        aggregate(acc[:, bass.ds(acc_at, CH)], h2_hi, h2_lo, q, h,
                                  lambda t: (hi_slots[:, bass.ds(at + t * CH, CH)],
                                             lo_slots[:, bass.ds(at + t * CH, CH)]), j == 0)\
                            .then_inc(adj_used, 1)

                block_of(NC - 1)
                with pe.If(turn_no >= 2):
                    gates(pe.snap(before_reg))
                pe.wait_ge(w_ready, 1)
                message(pe.snap(last_reg))
                turn_state(pe.snap(last_reg))

                def blocks_from(q):
                    with pe.If(lowest <= q):
                        block_of(q)
                        if q > 2:
                            blocks_from(q - 1)

                blocks_from(NC - 2)
                pe.reg_mov(before_reg, pe.snap(last_reg))
                pe.reg_mov(last_reg, turn_no)
            count = blocks_of(row_of(pe, NC - 1))
            for i in range(count):
                if i == count - 1:
                    gates(NC - 2)
                    turn_state(NC - 1)
                split_block(NB - count + i, NC - 1 - i, (NC - 1) % 2, i == 0)
                if i == 0:
                    gates(NC - 3)
                    message(NC - 2)
                    turn_state(NC - 2)
            gates_of_state(NC - 1)
            message(NC - 1)
            gates_of_message(NC - 1)


def kernel(x, adj, L0_gnn_h, L1_gnn_W_msg, L1_gnn_b_msg, L1_gnn_W_ih, L1_gnn_W_hh, L1_gnn_b_ih, L1_gnn_b_hh):
    import numpy as np
    import concourse.bacc as bacc
    from concourse.bass_utils import run_bass_kernel_spmd

    a = np.asarray
    blocks = a(adj).reshape(NC, CH, NC, JT, P).transpose(0, 2, 4, 3, 1)[:, ::-1].reshape(NA, P, GW)
    arrays = {
        "adj_in": blocks,
        "x_rows_in": a(x).reshape(NC, JT, P, P).transpose(0, 2, 1, 3).reshape(NC, P, HW),
        "x_cols_in": a(x).reshape(NC, CH, P).transpose(0, 2, 1),
        "h_cols_in": a(L0_gnn_h).reshape(NC, CH, P).transpose(0, 2, 1),
        "weights_in": np.concatenate([a(L1_gnn_W_msg), a(L1_gnn_W_ih), a(L1_gnn_W_hh)], 0)
                        .reshape(7, P, P).transpose(2, 0, 1),
        "biases_in": np.concatenate([a(L1_gnn_b_msg), a(L1_gnn_b_ih), a(L1_gnn_b_hh)], 0).reshape(7, P).transpose(1, 0),
        "identity_in": np.eye(P, dtype=np.float32),
    }
    arrays = {name: np.ascontiguousarray(v) for name, v in arrays.items()}
    nc = bacc.Bacc("TRN2", target_bir_lowering=False, num_devices=1)
    args = [nc.dram_tensor(name, v.shape, FP32, kind="ExternalInput").ap() for name, v in arrays.items()]
    out = nc.dram_tensor("out_cols", (NC, P, CH), FP32, kind="ExternalOutput").ap()
    gnn_program(nc, *args, out)
    r = run_bass_kernel_spmd(nc, [arrays], core_ids=[0])
    return np.ascontiguousarray(a(r.results[0]["out_cols"]).transpose(0, 2, 1).reshape(N, P))
```
